# Optimizing a Trainium2 kernel written in Bass

```python
import numpy as np
import jax
import jax.numpy as jnp

def _softmax(x, axis=-1):
    return jax.nn.softmax(x, axis=axis)

def _gelu(x):
    return jax.nn.gelu(x, approximate=True)

def _silu(x):
    return jax.nn.silu(x)

def _sigmoid(x):
    return jax.nn.sigmoid(x)

def _layernorm(x, axis=-1, eps=1e-05):
    m = jnp.mean(x, axis=axis, keepdims=True)
    v = jnp.var(x, axis=axis, keepdims=True)
    return (x - m) / jnp.sqrt(v + eps)

def _scatter_add(tgt, idx, src, axis=0):
    return tgt.at[idx].add(src)

def _segment_sum(src, seg, n):
    return jax.ops.segment_sum(src, seg, n)
kernel_name = 'mk_decoder_postln_d1_seqx_r4_efc486'

def setup_inputs(seed: int=0):
    np.random.seed(seed)
    _w = jnp.asarray

    def _rec_inputs():
        import jax
        import jax.numpy as jnp
        _rk = jax.random.key(seed)
        x = -0.000125 + 0.9999 * jax.random.normal(jax.random.fold_in(_rk, 1), (8, 256, 512), jnp.float32)
        _lenS = 256 - jax.random.randint(jax.random.fold_in(_rk, 7), (8,), 0, max(1, 256 // 4) + 1, jnp.int32)
        _lenS2 = 256 - jax.random.randint(jax.random.fold_in(_rk, 8), (8,), 0, max(1, 256 // 4) + 1, jnp.int32)
        _ctx_2048P = jax.random.normal(jax.random.fold_in(_rk, 11), (8, 16, 512), jnp.float32)
        _ctx_2048c = jax.random.dirichlet(jax.random.fold_in(_rk, 511), 0.3 * jnp.ones((16,), jnp.float32), (8, 256))
        _ctx_2048t = jnp.einsum('bsk,bkd->bsd', _ctx_2048c, _ctx_2048P)
        _ctx_2048t = _ctx_2048t * jax.lax.rsqrt(jnp.mean(jnp.square(_ctx_2048t)) + 1e-12) * 0.953939
        ctx_2048 = -1.52775e-05 + 0.999936 * (_ctx_2048t + 0.3 * jax.random.normal(jax.random.fold_in(_rk, 611), (8, 256, 512), jnp.float32))
        return (x, ctx_2048)
    x, ctx_2048 = _rec_inputs()

    def _L0_attn_setup():
        import jax, jax.numpy as jnp
        import numpy as np
        B, T, E = (4, 512, 512)
        H, KV = (16, 4)
        G = H // KV
        D = E // H
        key = jax.random.key(seed)
        kx, kq, kk, kv, ko = jax.random.split(key, 5)
        s = 1.0 / np.sqrt(E).astype(np.float32)
        x = jax.random.normal(kx, (B, T, E), jnp.float32)
        Wq = jax.random.normal(kq, (E, H * D), jnp.float32) * s
        Wk = jax.random.normal(kk, (E, KV * D), jnp.float32) * s
        Wv = jax.random.normal(kv, (E, KV * D), jnp.float32) * s
        Wo = jax.random.normal(ko, (H * D, E), jnp.float32) * s
        return {'x': x, 'Wq': Wq, 'Wk': Wk, 'Wv': Wv, 'Wo': Wo}
    _L0_attn_all = _L0_attn_setup()
    _L0_attn_in = {k: v for k, v in _L0_attn_all.items() if k in ('Wq', 'Wk', 'Wv', 'Wo')}
    del _L0_attn_all

    def _L0_xattn_setup():
        import jax, jax.numpy as jnp
        import numpy as np
        B, S, D, H = (4, 1024, 512, 16)
        HD = D // H
        key = jax.random.key(seed)
        ks = jax.random.split(key, 12)
        sc = 1.0 / np.sqrt(D)
        inp = {'q': jax.random.normal(ks[0], (B, S, D), jnp.float32), 'k': jax.random.normal(ks[1], (B, S, D), jnp.float32), 'v': jax.random.normal(ks[2], (B, S, D), jnp.float32), 'Wq': jax.random.normal(ks[3], (D, D), jnp.float32) * sc, 'bq': jnp.zeros((D,), jnp.float32), 'Wk': jax.random.normal(ks[4], (D, D), jnp.float32) * sc, 'bk': jnp.zeros((D,), jnp.float32), 'Wv': jax.random.normal(ks[5], (D, D), jnp.float32) * sc, 'bv': jnp.zeros((D,), jnp.float32), 'Wo': jax.random.normal(ks[6], (D, D), jnp.float32) * sc, 'bo': jnp.zeros((D,), jnp.float32)}
        return inp
    _L0_xattn_all = _L0_xattn_setup()
    _L0_xattn_in = {k: v for k, v in _L0_xattn_all.items() if k in ('Wq', 'bq', 'Wk', 'bk', 'Wv', 'bv', 'Wo', 'bo')}
    del _L0_xattn_all

    def _L0_ffn_setup():
        import jax, jax.numpy as jnp
        import numpy as np
        B, S, H, I, E, F, K, R, TOPK = (1, 256, 512, 352, 64, 8, 8, 8, 6)
        ISH = 2 * I

        def _fused_linear(x, W, qa, qb, scale, w):
            out = x @ W.T
            a = jnp.einsum('th,krh->tkr', x, qa)
            b = jnp.einsum('tkr,khr->tkh', a, qb)
            mix = jnp.einsum('tkh,tk->th', b, w)
            return out + scale[None, :] * mix

        def _moe_forward(hidden_states, gate_weight, inv_mapping, mask_up_W, gate_W, gate_qa, gate_qb, gate_scale, up_W, up_qa, up_qb, up_scale, down_W, down_qa, down_qb, down_scale, sh_gate_W, sh_up_W, sh_down_W):
            b, s, h = hidden_states.shape
            x = hidden_states.reshape(-1, h)
            T = x.shape[0]
            scores = jax.nn.softmax(x @ gate_weight.T, axis=-1)
            topk_w, topk_idx = jax.lax.top_k(scores, TOPK)
            w_dense = jnp.zeros((T, E), x.dtype).at[jnp.arange(T)[:, None], topk_idx].add(topk_w)
            flat = w_dense[:, inv_mapping]
            scalar = flat.sum(-1)
            soft = jax.nn.softmax(jnp.where(flat == 0, -1000000000.0, flat), axis=-1)

            def expert(muW, gW, gqa, gqb, gs, uW, uqa, uqb, us, dW, dqa, dqb, ds, w):
                xe = x + w @ muW.T
                gate = jax.nn.silu(_fused_linear(xe, gW, gqa, gqb, gs, w))
                up = _fused_linear(xe, uW, uqa, uqb, us, w)
                return _fused_linear(gate * up, dW, dqa, dqb, ds, w)
            outs = jax.vmap(expert, in_axes=(0,) * 13 + (1,))(mask_up_W, gate_W, gate_qa, gate_qb, gate_scale, up_W, up_qa, up_qb, up_scale, down_W, down_qa, down_qb, down_scale, soft)
            y = jnp.einsum('fth,tf->th', outs, scalar).reshape(b, s, h)
            sh = jax.nn.silu(hidden_states @ sh_gate_W.T) * (hidden_states @ sh_up_W.T) @ sh_down_W.T
            return y + sh
        key = jax.random.key(seed)
        ks = jax.random.split(key, 20)
        g = lambda k, shape, s=0.02: jax.random.normal(k, shape, jnp.float32) * s
        return {'hidden_states': jax.random.normal(ks[0], (B, S, H), jnp.float32), 'gate_weight': g(ks[1], (E, H)), 'inv_mapping': jnp.arange(E, dtype=jnp.int32).reshape(F, K), 'mask_up_W': g(ks[2], (F, H, K)), 'gate_W': g(ks[3], (F, I, H)), 'gate_qa': g(ks[4], (F, K, R, H)), 'gate_qb': g(ks[5], (F, K, I, R)), 'gate_scale': jnp.full((F, I), 0.1, jnp.float32), 'up_W': g(ks[6], (F, I, H)), 'up_qa': g(ks[7], (F, K, R, H)), 'up_qb': g(ks[8], (F, K, I, R)), 'up_scale': jnp.full((F, I), 0.1, jnp.float32), 'down_W': g(ks[9], (F, H, I)), 'down_qa': g(ks[10], (F, K, R, I)), 'down_qb': g(ks[11], (F, K, H, R)), 'down_scale': jnp.full((F, H), 0.1, jnp.float32), 'sh_gate_W': g(ks[12], (ISH, H)), 'sh_up_W': g(ks[13], (ISH, H)), 'sh_down_W': g(ks[14], (H, ISH))}
    _L0_ffn_all = _L0_ffn_setup()
    _L0_ffn_in = {k: v for k, v in _L0_ffn_all.items() if k in ('gate_weight', 'inv_mapping', 'mask_up_W', 'gate_W', 'gate_qa', 'gate_qb', 'gate_scale', 'up_W', 'up_qa', 'up_qb', 'up_scale', 'down_W', 'down_qa', 'down_qb', 'down_scale', 'sh_gate_W', 'sh_up_W', 'sh_down_W')}
    del _L0_ffn_all
    return {'x': x, 'ctx_2048': ctx_2048, 'L0_attn_Wq': _L0_attn_in['Wq'], 'L0_attn_Wk': _L0_attn_in['Wk'], 'L0_attn_Wv': _L0_attn_in['Wv'], 'L0_attn_Wo': _L0_attn_in['Wo'], 'L0_xattn_Wq': _L0_xattn_in['Wq'], 'L0_xattn_bq': _L0_xattn_in['bq'], 'L0_xattn_Wk': _L0_xattn_in['Wk'], 'L0_xattn_bk': _L0_xattn_in['bk'], 'L0_xattn_Wv': _L0_xattn_in['Wv'], 'L0_xattn_bv': _L0_xattn_in['bv'], 'L0_xattn_Wo': _L0_xattn_in['Wo'], 'L0_xattn_bo': _L0_xattn_in['bo'], 'L0_ffn_gate_weight': _L0_ffn_in['gate_weight'], 'L0_ffn_inv_mapping': _L0_ffn_in['inv_mapping'], 'L0_ffn_mask_up_W': _L0_ffn_in['mask_up_W'], 'L0_ffn_gate_W': _L0_ffn_in['gate_W'], 'L0_ffn_gate_qa': _L0_ffn_in['gate_qa'], 'L0_ffn_gate_qb': _L0_ffn_in['gate_qb'], 'L0_ffn_gate_scale': _L0_ffn_in['gate_scale'], 'L0_ffn_up_W': _L0_ffn_in['up_W'], 'L0_ffn_up_qa': _L0_ffn_in['up_qa'], 'L0_ffn_up_qb': _L0_ffn_in['up_qb'], 'L0_ffn_up_scale': _L0_ffn_in['up_scale'], 'L0_ffn_down_W': _L0_ffn_in['down_W'], 'L0_ffn_down_qa': _L0_ffn_in['down_qa'], 'L0_ffn_down_qb': _L0_ffn_in['down_qb'], 'L0_ffn_down_scale': _L0_ffn_in['down_scale'], 'L0_ffn_sh_gate_W': _L0_ffn_in['sh_gate_W'], 'L0_ffn_sh_up_W': _L0_ffn_in['sh_up_W'], 'L0_ffn_sh_down_W': _L0_ffn_in['sh_down_W']}

def reference(x, ctx_2048, L0_attn_Wq, L0_attn_Wk, L0_attn_Wv, L0_attn_Wo, L0_xattn_Wq, L0_xattn_bq, L0_xattn_Wk, L0_xattn_bk, L0_xattn_Wv, L0_xattn_bv, L0_xattn_Wo, L0_xattn_bo, L0_ffn_gate_weight, L0_ffn_inv_mapping, L0_ffn_mask_up_W, L0_ffn_gate_W, L0_ffn_gate_qa, L0_ffn_gate_qb, L0_ffn_gate_scale, L0_ffn_up_W, L0_ffn_up_qa, L0_ffn_up_qb, L0_ffn_up_scale, L0_ffn_down_W, L0_ffn_down_qa, L0_ffn_down_qb, L0_ffn_down_scale, L0_ffn_sh_gate_W, L0_ffn_sh_up_W, L0_ffn_sh_down_W):
    import jax
    import jax.numpy as jnp

    def _L0_attn_ref(x, Wq, Wk, Wv, Wo):
        import jax, jax.numpy as jnp
        import numpy as np
        B, T, E = (4, 512, 512)
        H, KV = (16, 4)
        G = H // KV
        D = E // H
        b, t, _ = x.shape
        scale = 1.0 / np.sqrt(D).astype(np.float32)
        q = (x @ Wq).reshape(b, t, KV, G, D)
        k = (x @ Wk).reshape(b, t, KV, D)
        v = (x @ Wv).reshape(b, t, KV, D)
        scores = jnp.einsum('bqhgd,bkhd->bhgqk', q, k) * scale
        causal_mask = jnp.tril(jnp.ones((t, t), dtype=bool))
        scores = jnp.where(causal_mask, scores, -jnp.inf)
        w = jax.nn.softmax(scores, axis=-1)
        y = jnp.einsum('bhgqk,bkhd->bqhgd', w, v)
        y = y.reshape(b, t, H * D)
        return y @ Wo

    def _L0_xattn_ref(q, k, v, Wq, bq, Wk, bk, Wv, bv, Wo, bo):
        import jax, jax.numpy as jnp
        import numpy as np
        B, S, D, H = (4, 1024, 512, 16)
        HD = D // H
        bs, sl, nf = q.shape
        Q = (q @ Wq.T + bq).reshape(bs, sl, H, HD)
        K = (k @ Wk.T + bk).reshape(bs, sl, H, HD)
        V = (v @ Wv.T + bv).reshape(bs, sl, H, HD)
        score = jnp.einsum('bshd,bsgd->bshg', Q, K)
        weight = jax.nn.softmax(score, axis=-1)
        attn = jnp.einsum('bshg,bsgd->bshd', weight, V).reshape(bs, sl, nf)
        return attn @ Wo.T + bo

    def _L0_ffn_ref(hidden_states, gate_weight, inv_mapping, mask_up_W, gate_W, gate_qa, gate_qb, gate_scale, up_W, up_qa, up_qb, up_scale, down_W, down_qa, down_qb, down_scale, sh_gate_W, sh_up_W, sh_down_W):
        import jax, jax.numpy as jnp
        import numpy as np
        B, S, H, I, E, F, K, R, TOPK = (1, 256, 512, 352, 64, 8, 8, 8, 6)
        ISH = 2 * I

        def _fused_linear(x, W, qa, qb, scale, w):
            out = x @ W.T
            a = jnp.einsum('th,krh->tkr', x, qa)
            b = jnp.einsum('tkr,khr->tkh', a, qb)
            mix = jnp.einsum('tkh,tk->th', b, w)
            return out + scale[None, :] * mix

        def _moe_forward(hidden_states, gate_weight, inv_mapping, mask_up_W, gate_W, gate_qa, gate_qb, gate_scale, up_W, up_qa, up_qb, up_scale, down_W, down_qa, down_qb, down_scale, sh_gate_W, sh_up_W, sh_down_W):
            b, s, h = hidden_states.shape
            x = hidden_states.reshape(-1, h)
            T = x.shape[0]
            scores = jax.nn.softmax(x @ gate_weight.T, axis=-1)
            topk_w, topk_idx = jax.lax.top_k(scores, TOPK)
            w_dense = jnp.zeros((T, E), x.dtype).at[jnp.arange(T)[:, None], topk_idx].add(topk_w)
            flat = w_dense[:, inv_mapping]
            scalar = flat.sum(-1)
            soft = jax.nn.softmax(jnp.where(flat == 0, -1000000000.0, flat), axis=-1)

            def expert(muW, gW, gqa, gqb, gs, uW, uqa, uqb, us, dW, dqa, dqb, ds, w):
                xe = x + w @ muW.T
                gate = jax.nn.silu(_fused_linear(xe, gW, gqa, gqb, gs, w))
                up = _fused_linear(xe, uW, uqa, uqb, us, w)
                return _fused_linear(gate * up, dW, dqa, dqb, ds, w)
            outs = jax.vmap(expert, in_axes=(0,) * 13 + (1,))(mask_up_W, gate_W, gate_qa, gate_qb, gate_scale, up_W, up_qa, up_qb, up_scale, down_W, down_qa, down_qb, down_scale, soft)
            y = jnp.einsum('fth,tf->th', outs, scalar).reshape(b, s, h)
            sh = jax.nn.silu(hidden_states @ sh_gate_W.T) * (hidden_states @ sh_up_W.T) @ sh_down_W.T
            return y + sh
        return _moe_forward(hidden_states, gate_weight, inv_mapping, mask_up_W, gate_W, gate_qa, gate_qb, gate_scale, up_W, up_qa, up_qb, up_scale, down_W, down_qa, down_qb, down_scale, sh_gate_W, sh_up_W, sh_down_W)
    x = _layernorm(x + _L0_attn_ref(x, L0_attn_Wq, L0_attn_Wk, L0_attn_Wv, L0_attn_Wo), axis=-1)
    x = _layernorm(x + _L0_xattn_ref(x, ctx_2048, ctx_2048, L0_xattn_Wq, L0_xattn_bq, L0_xattn_Wk, L0_xattn_bk, L0_xattn_Wv, L0_xattn_bv, L0_xattn_Wo, L0_xattn_bo), axis=-1)
    x = _layernorm(x + _L0_ffn_ref(x, L0_ffn_gate_weight, L0_ffn_inv_mapping, L0_ffn_mask_up_W, L0_ffn_gate_W, L0_ffn_gate_qa, L0_ffn_gate_qb, L0_ffn_gate_scale, L0_ffn_up_W, L0_ffn_up_qa, L0_ffn_up_qb, L0_ffn_up_scale, L0_ffn_down_W, L0_ffn_down_qa, L0_ffn_down_qb, L0_ffn_down_scale, L0_ffn_sh_gate_W, L0_ffn_sh_up_W, L0_ffn_sh_down_W), axis=-1)
    return x

_drawn_inputs = setup_inputs


def setup_inputs(seed=0):
    import zlib

    import numpy as np

    out = dict(_drawn_inputs(seed))
    spreads = {'L0_xattn_bq': (0.0, 0.1),
     'L0_xattn_bk': (0.0, 0.1),
     'L0_xattn_bv': (0.0, 0.1),
     'L0_xattn_bo': (0.0, 0.1),
     'L0_ffn_gate_scale': (0.10000000149011612, 0.6),
     'L0_ffn_up_scale': (0.10000000149011612, 0.6),
     'L0_ffn_down_scale': (0.10000000149011612, 0.6)}
    factors = {'L0_ffn_gate_weight': 8.0,
     'L0_ffn_mask_up_W': 8.0,
     'L0_ffn_gate_W': 7.287,
     'L0_ffn_gate_qa': 8.0,
     'L0_ffn_gate_qb': 8.0,
     'L0_ffn_up_W': 7.051,
     'L0_ffn_up_qa': 21.667,
     'L0_ffn_up_qb': 21.843,
     'L0_ffn_down_W': 7.152,
     'L0_ffn_down_qa': 8.0,
     'L0_ffn_down_qb': 8.0,
     'L0_ffn_sh_gate_W': 8.0,
     'L0_ffn_sh_up_W': 8.0,
     'L0_ffn_sh_down_W': 8.0}
    for name, (base, spread) in spreads.items():
        noise = np.random.default_rng([zlib.crc32(name.encode()), seed]).standard_normal(out[name].shape)
        drawn = base * np.exp(spread * noise) if base else spread * noise
        out[name] = jnp.asarray(drawn.astype(out[name].dtype))
    for name, factor in factors.items():
        out[name] = (out[name] * factor).astype(out[name].dtype)
    return out
```

```python
from contextlib import ExitStack

import concourse.bass as bass
from concourse import mybir

ALU = mybir.AluOpType
ACT = mybir.ActivationFunctionType
F32, F32R = mybir.dt.float32, mybir.dt.float32r
AX_X = mybir.AxisListType.X

P = 128
B, S, D = 8, 256, 512
T = B * S
NT = T // P
KC = D // P
TB = 512
NB = T // TB
F, K8, R8, I = 8, 8, 8, 352
NF = F
KR = K8 * R8
E = F * K8
TOPK = 6
ITILES = [128, 128, 96]
NI = len(ITILES)
EPS = 1e-5

KV, G, HD = 4, 4, 32
NEG = -1e30
NH = KV * G
ROWS = 104
NG = S // 8
NQ = NG // 4


def after(eng, s, count):
    if not (isinstance(count, int) and count <= 0):
        eng.wait_ge(s, count)


def over_batches(eng, body):
    body(0)
    with eng.Fori(1, B) as b:
        body(b)


class Steps:

    def __init__(self, eng, sem, per, turn):
        self.eng, self.sem, self.per, self.turn, self.n = eng, sem, per, turn, 0

    def did(self, instruction):
        instruction.then_inc(self.sem, 1)
        self.n += 1

    def settle(self):
        self.eng.wait_ge(self.sem, self.turn * self.per + self.n)

    def close(self):
        assert self.n == self.per, self.n


def alone(eng, past):
    eng.sem_inc(past, 1)


class Splitter:

    def __init__(self, nc, ctx):
        self.nc = nc
        self.landed = [ctx.enter_context(nc.semaphore(f"weights_landed{n}")) for n in range(4)]
        self.loads = [0] * 4
        self.high, self.low = ctx.enter_context(nc.semaphore("split_high")), ctx.enter_context(nc.semaphore("split_low"))
        self.done = 0

    def split(self, loads):
        nc, before = self.nc, self.done
        with ExitStack() as ctx:
            raws = [ctx.enter_context(nc.sbuf_tensor(f"land_{hi.tensor.name}", list(hi.shape), F32)) for _, hi, _ in loads]
            block = ctx.enter_context(nc.Block())
            for n in range(len(loads)):
                self.loads[n] += 1

            @block.sync
            def _(sp):
                for n, (src, _, _) in enumerate(loads):
                    sp.dma_start(raws[n][:], src).then_inc(self.landed[n], 16)

            @block.scalar
            def _(act):
                for n, (_, hi, _) in enumerate(loads):
                    act.wait_ge(self.landed[n], 16 * self.loads[n])
                    nc.scalar.activation(hi, raws[n][:], ACT.Copy).then_inc(self.high, 1)

            @block.vector
            def _(dve):
                for n, (_, hi, lo) in enumerate(loads):
                    dve.wait_ge(self.high, before + n + 1)
                    nc.vector.tensor_tensor(lo, raws[n][:], hi.bitcast(F32), ALU.subtract).then_inc(self.low, 1)
                dve.wait_ge(self.low, before + len(loads))
            self.done += len(loads)


def attention(nc, splitter, A, ident, x2T, xtok):
    with ExitStack() as ctx:
        def sb(name, shape, dt=F32):
            return ctx.enter_context(nc.sbuf_tensor(name, shape, dt))

        def sem(name):
            return ctx.enter_context(nc.semaphore(name))

        WQH, WQL = sb("WQH", [P, KC, D], F32R), sb("WQL", [P, KC, D], F32R)
        WKH, WKL = sb("WKH", [P, KC, P], F32R), sb("WKL", [P, KC, P], F32R)
        WOH, WOL = sb("WOH", [P, G, D], F32R), sb("WOL", [P, G, D], F32R)
        splitter.split([(A["wq"], WQH[:], WQL[:]), (A["wk"], WKH[:], WKL[:]), (A["wo"], WOH[:], WOL[:])])
        wv = sb("wv_sb", [P, KC, P])
        identR = sb("identR", [P, P], F32R)
        mask_f = sb("mask_f", [P, KV, P + S])
        mask0, mask1 = sb("mask0", [P, KV, P], F32R), sb("mask1", [P, 2, S], F32R)
        xT, x_in = sb("xT_raw", [P, KC, S]), sb("x_raw", [P, 2, D])
        XH, XL = sb("aXH", [P, KC, S], F32R), sb("aXL", [P, KC, S], F32R)
        QH, QL = sb("QH", [P, G, S], F32R), sb("QL", [P, G, S], F32R)
        KH, KL = sb("KH", [P, KV, S], F32R), sb("KL", [P, KV, S], F32R)
        V = sb("V", [P, 2, P])
        p0, p1 = sb("p0", [P, 2, KV, P]), sb("p1", [P, 2, KV, S])
        PT = sb("PT", [P, 2, KV, 3 * P])
        OH, OL = sb("OH", [P, G, S], F32R), sb("OL", [P, G, S], F32R)
        mx, nm, sums, rinv = (sb(n, [P, 2, 8]) for n in ("mx", "nm", "sums", "rinv"))
        r, xs = sb("r", [P, 2, D]), sb("xs", [P, 2, D])
        st, mv, ve, rstd, half = sb("st", [P, 2, 6]), sb("mv", [P, 2, 2]), sb("ve", [P, 2]), sb("rstd", [P, 2]), sb("half", [P, 2])
        s_ps = [ctx.enter_context(nc.psum_tensor(f"s_ps{i}", [P, 512], F32)) for i in range(3)]
        t_ps = [ctx.enter_context(nc.psum_tensor(f"t_ps{i}", [P, 4, P], F32)) for i in range(3)]
        j_ps = [ctx.enter_context(nc.psum_tensor(f"j_ps{i}", [P, 512], F32)) for i in range(2)]

        l_w, l_x, l_xt = sem("l_w"), sem("l_x"), sem("l_xt")
        consts, const_r, past = sem("consts"), sem("const_r"), sem("past")
        xh_rdy, xl_rdy = sem("a_xh"), sem("a_xl")
        proj_done, hi_rdy, lo_rdy, v_rdy = sem("proj_done"), sem("hi_rdy"), sem("lo_rdy"), sem("v_rdy")
        s_done, max_rdy, exp_done, rinv_rdy, norm_rdy = (sem(n) for n in ("s_done", "max_rdy", "exp_done", "rinv_rdy", "norm_rdy"))
        t_done, pt_act, pt_dve, o_done, oh_rdy, ol_rdy = (sem(n) for n in ("t_done", "pt_act", "pt_dve", "o_done", "oh_rdy", "ol_rdy"))
        wo_done, ve_rdy, rstd_rdy, xs_rdy, xt_done, xt_act, xt_dve, xtok_rdy = (
            sem(n) for n in ("wo_done", "ve_rdy", "rstd_rdy", "xs_rdy", "xt_done", "xt_act", "xt_dve", "xtok_rdy"))
        dve_steps = sem("dve_steps")
        NPJ = G + 2
        SCALE = HD ** -0.5
        block = ctx.enter_context(nc.Block())

        @block.sync
        def _(sp):
            sp.dma_start(wv[:], A["wv"]).then_inc(l_w, 16)

            def batch(b):
                after(sp, xl_rdy, b)
                after(sp, v_rdy, b)
                sp.dma_start(xT[:], A["xT"][:, :, bass.ds(b * S, S)]).then_inc(l_xt, 16)
                after(sp, ve_rdy, 2 * b)
                sp.dma_start(x_in[:], A["x"][bass.ds(b * S, S), :].rearrange("(i p) n -> p i n", p=P)).then_inc(l_x, 16)
            over_batches(sp, batch)

        @block.gpsimd
        def _(pool):
            nc.gpsimd.memset(mask_f[:], 0.0).then_inc(consts, 1)
            nc.gpsimd.memset(half[:], -0.5).then_inc(consts, 1)
            nc.gpsimd.memset(KH[:].bitcast(F32), 0.0).then_inc(consts, 1)
            nc.gpsimd.memset(KL[:].bitcast(F32), 0.0).then_inc(consts, 1)
            pool.wait_ge(consts, 1)
            nc.gpsimd.affine_select(out=mask_f[:, :, 0:P], in_=mask_f[:, :, 0:P], compare_op=ALU.is_ge, fill=NEG,
                                    base=0, pattern=[[0, KV], [-1, P]], channel_multiplier=1).then_inc(consts, 1)
            nc.gpsimd.affine_select(out=mask_f[:, 0:2, P:P + S], in_=mask_f[:, 0:2, P:P + S], compare_op=ALU.is_ge, fill=NEG,
                                    base=P, pattern=[[0, 2], [-1, S]], channel_multiplier=1).then_inc(consts, 1)

            def batch(b):
                for g in range(G):
                    u = g % 2
                    after(pool, rinv_rdy, G * b + g + 1)
                    nc.gpsimd.tensor_tensor(p0[:, u], p0[:, u], rinv[:, u, 0:4].unsqueeze(2).to_broadcast([P, KV, P]), ALU.mult)
                    nc.gpsimd.tensor_tensor(p1[:, u], p1[:, u], rinv[:, u, 4:8].unsqueeze(2).to_broadcast([P, KV, S]),
                                            ALU.mult).then_inc(norm_rdy, 1)
                for i in range(2):
                    after(pool, ve_rdy, 2 * b + i + 1)
                    nc.gpsimd.tensor_tensor(rstd[:, i:i + 1], ve[:, i:i + 1], half[:, i:i + 1], ALU.pow).then_inc(rstd_rdy, 1)
                for i in range(2):
                    after(pool, xs_rdy, 2 * b + i + 1)
                    alone(pool, past)
                    nc.gpsimd.tensor_copy(xtok[:, bass.ds(2 * b + i, 1), :], xs[:, i:i + 1, :]).then_inc(xtok_rdy, 1)
            over_batches(pool, batch)

        @block.scalar
        def _(act):
            copy = lambda out, src: nc.scalar.activation(out, src, ACT.Copy)
            act.wait_ge(consts, 6)
            copy(mask0[:], mask_f[:, :, 0:P]).then_inc(const_r, 1)
            copy(mask1[:], mask_f[:, 0:2, P:P + S]).then_inc(const_r, 1)
            copy(identR[:], ident[:]).then_inc(const_r, 1)

            def batch(b):
                after(act, l_xt, 16 * (b + 1))
                after(act, proj_done, NPJ * b)
                copy(XH[:], xT[:]).then_inc(xh_rdy, 1)
                after(act, proj_done, NPJ * b + 1)
                after(act, s_done, G * b)
                for kv in range(KV):
                    rows = slice(HD * kv, HD * kv + HD)
                    last = copy(KH[rows, kv, :], j_ps[0][rows, 0:S])
                last.then_inc(hi_rdy, 1)
                for g in range(G):
                    after(act, proj_done, NPJ * b + g + 2)
                    copy(QH[:, g, :], j_ps[(g + 1) % 2][:, 0:S]).then_inc(hi_rdy, 1)
                after(act, proj_done, NPJ * b + NPJ)
                after(act, o_done, G * b)
                copy(V[:].rearrange("p i v -> p (i v)"), j_ps[1][:, 0:S]).then_inc(v_rdy, 1)

                def pt_copy(g):
                    after(act, t_done, G * b + g + 1)
                    u = g % 2
                    copy(PT[:, u, :, 0:P], t_ps[0][:])
                    copy(PT[:, u, :, 2 * P:3 * P], t_ps[2][:]).then_inc(pt_act, 1)

                def o_copy(g):
                    after(act, o_done, G * b + g + 1)
                    copy(OH[:, g, :], j_ps[g % 2][:, 0:S]).then_inc(oh_rdy, 1)

                for g in range(G):
                    u = g % 2
                    after(act, max_rdy, G * b + g + 1)
                    for kv in range(KV):
                        nc.scalar.activation(p0[:, u, kv, :], s_ps[0][:, kv * P:(kv + 1) * P], ACT.Exp,
                                             bias=nm[:, u, kv:kv + 1], scale=SCALE, accum_out=sums[:, u, kv:kv + 1])
                    for kv in range(KV):
                        at = kv % 2 * S
                        last = nc.scalar.activation(p1[:, u, kv, :], s_ps[1 + kv // 2][:, at:at + S], ACT.Exp,
                                                    bias=nm[:, u, 4 + kv:5 + kv], scale=SCALE, accum_out=sums[:, u, 4 + kv:5 + kv])
                    last.then_inc(exp_done, 1)
                    if g >= 1:
                        pt_copy(g - 1)
                    if g >= 2:
                        o_copy(g - 2)
                pt_copy(G - 1)
                o_copy(G - 2)
                o_copy(G - 1)
                for i in range(2):
                    after(act, xt_done, 2 * b + i + 1)
                    alone(act, past)
                    copy(x2T[:, 0:2, bass.ds(b * S + i * P, P)], t_ps[i][:, 0:2, :]).then_inc(xt_act, 1)
            over_batches(act, batch)

        @block.vector
        def _(dve):
            sub = lambda out, a, b: nc.vector.tensor_tensor(out, a, b, ALU.subtract)

            def batch(b):
                own = Steps(dve, dve_steps, G + 2 * 3, b)
                after(dve, xh_rdy, b + 1)
                sub(XL[:], xT[:], XH[:].bitcast(F32)).then_inc(xl_rdy, 1)
                after(dve, hi_rdy, (G + 1) * b + 1)
                for kv in range(KV):
                    rows = slice(HD * kv, HD * kv + HD)
                    last = sub(KL[rows, kv, :], j_ps[0][rows, 0:S], KH[rows, kv, :].bitcast(F32))
                last.then_inc(lo_rdy, 1)
                for g in range(G):
                    after(dve, hi_rdy, (G + 1) * b + g + 2)
                    sub(QL[:, g, :], j_ps[(g + 1) % 2][:, 0:S], QH[:, g, :].bitcast(F32)).then_inc(lo_rdy, 1)

                def rest(g):
                    u = g % 2
                    after(dve, exp_done, G * b + g + 1)
                    nc.vector.reciprocal(rinv[:, u, :], sums[:, u, :]).then_inc(rinv_rdy, 1)

                def pt_copy(g):
                    after(dve, t_done, G * b + g + 1)
                    nc.vector.tensor_copy(PT[:, g % 2, :, P:2 * P], t_ps[1][:]).then_inc(pt_dve, 1)

                def o_sub(g):
                    after(dve, oh_rdy, G * b + g + 1)
                    sub(OL[:, g, :], j_ps[g % 2][:, 0:S], OH[:, g, :].bitcast(F32)).then_inc(ol_rdy, 1)

                for g in range(G):
                    u = g % 2
                    after(dve, s_done, G * b + g + 1)
                    nc.vector.reduce_max(mx[:, u, 0:4], s_ps[0][:].rearrange("p (v s) -> p v s", v=KV), AX_X)
                    nc.vector.reduce_max(mx[:, u, 4:6], s_ps[1][:].rearrange("p (v s) -> p v s", v=2), AX_X)
                    own.did(nc.vector.reduce_max(mx[:, u, 6:8], s_ps[2][:].rearrange("p (v s) -> p v s", v=2), AX_X))
                    own.settle()
                    nc.vector.tensor_scalar(nm[:, u, :], mx[:, u, :], -SCALE, None, ALU.mult).then_inc(max_rdy, 1)
                    if g >= 1:
                        pt_copy(g - 1)
                    rest(g)
                    if g >= 2:
                        o_sub(g - 2)
                pt_copy(G - 1)
                o_sub(G - 2)
                o_sub(G - 1)
                after(dve, l_x, 16 * (b + 1))
                for i in range(2):
                    after(dve, wo_done, 2 * b + i + 1)
                    own.did(nc.vector.tensor_tensor(r[:, i, :], j_ps[i][:], x_in[:, i, :], ALU.add))
                    own.settle()
                    own.did(nc.vector.bn_stats(st[:, i, :], r[:, i, :]))
                    own.settle()
                    alone(dve, past)
                    own.did(nc.vector.bn_aggr(mv[:, i, :], st[:, i, :]))
                    own.settle()
                    nc.vector.tensor_scalar(ve[:, i:i + 1], mv[:, i, 1:2], EPS, None, ALU.add).then_inc(ve_rdy, 1)
                for i in range(2):
                    after(dve, rstd_rdy, 2 * b + i + 1)
                    after(dve, xtok_rdy, 2 * b)
                    after(dve, xt_done, 2 * b)
                    nc.vector.tensor_scalar(xs[:, i, :], r[:, i, :], mv[:, i, 0:1], rstd[:, i:i + 1],
                                            ALU.subtract, ALU.mult).then_inc(xs_rdy, 1)
                for i in range(2):
                    after(dve, xt_act, 2 * b + i + 1)
                    alone(dve, past)
                    nc.vector.tensor_copy(x2T[:, 2:4, bass.ds(b * S + i * P, P)], t_ps[i][:, 2:4, :]).then_inc(xt_dve, 1)
                own.close()
            over_batches(dve, batch)

        @block.tensor
        def _(pe):
            mm = nc.tensor.matmul

            def three(out, wh, wl, xh, xl, first, last):
                mm(out, wh, xh, start=first, stop=False)
                mm(out, wh, xl, start=False, stop=False)
                return mm(out, wl, xh, start=False, stop=last)

            pe.wait_ge(l_w, 16)
            pe.wait_ge(const_r, 3)

            def batch(b):
                after(pe, xl_rdy, b + 1)
                after(pe, ve_rdy, 2 * b)
                for k in range(KC):
                    last = three(j_ps[0][:, 0:S], WKH[:, k, :], WKL[:, k, :], XH[:, k, :], XL[:, k, :], k == 0, k == KC - 1)
                last.then_inc(proj_done, 1)
                for g in range(G):
                    if g >= 1:
                        after(pe, lo_rdy, (G + 1) * b + g)
                    for k in range(KC):
                        c = slice(g * P, (g + 1) * P)
                        last = three(j_ps[(g + 1) % 2][:, 0:S], WQH[:, k, c], WQL[:, k, c], XH[:, k, :], XL[:, k, :], k == 0, k == KC - 1)
                    last.then_inc(proj_done, 1)
                after(pe, lo_rdy, (G + 1) * b + G)
                for i in range(2):
                    for k in range(KC):
                        last = mm(j_ps[1][:, i * P:(i + 1) * P], xT[:, k, i * P:(i + 1) * P], wv[:, k, :],
                                  start=(k == 0), stop=(k == KC - 1), skip_group_check=True)
                last.then_inc(proj_done, 1)

                def scores(g):
                    if g >= 1:
                        after(pe, exp_done, G * b + g)
                    after(pe, lo_rdy, (G + 1) * b + g + 2)
                    for bank, i, kv, keys, m in ((0, 0, slice(0, 4), slice(0, P), mask0), (1, 1, slice(0, 2), slice(0, S), mask1),
                                                 (2, 1, slice(2, 4), slice(0, S), mask1)):
                        q = slice(i * P, (i + 1) * P)
                        out = s_ps[bank][:].rearrange("p (v s) -> p v s", v=4 if bank == 0 else 2)
                        three(out, QH[:, g, q], QL[:, g, q], KH[:, kv, keys], KL[:, kv, keys], True, False)
                        last = mm(out, identR[:], m[:], start=False, stop=True)
                    last.then_inc(s_done, 1)

                def turn(g):
                    u = g % 2
                    after(pe, norm_rdy, G * b + g + 1)
                    if g >= 1:
                        after(pe, pt_act, G * b + g)
                        after(pe, pt_dve, G * b + g)
                    for kv in range(KV):
                        nc.tensor.transpose(t_ps[0][:, kv, :], p0[:, u, kv, :], ident[:])
                        nc.tensor.transpose(t_ps[1][:, kv, :], p1[:, u, kv, 0:P], ident[:])
                        last = nc.tensor.transpose(t_ps[2][:, kv, :], p1[:, u, kv, P:S], ident[:])
                    last.then_inc(t_done, 1)

                def values(g):
                    u = g % 2
                    after(pe, pt_act, G * b + g + 1)
                    after(pe, pt_dve, G * b + g + 1)
                    if g < 2:
                        after(pe, v_rdy, b + 1)
                    else:
                        after(pe, ol_rdy, G * b + g - 1)
                    for kv in range(KV):
                        mm(j_ps[g % 2][HD * kv:HD * kv + HD, 0:S], V[:, 0, HD * kv:HD * kv + HD], PT[:, u, kv, 0:S],
                           start=True, stop=False)
                    for kv in range(KV):
                        last = mm(j_ps[g % 2][HD * kv:HD * kv + HD, P:S], V[:, 1, HD * kv:HD * kv + HD], PT[:, u, kv, S:S + P],
                                  start=False, stop=True)
                    last.then_inc(o_done, 1)

                after(pe, xt_dve, 2 * b)
                scores(0)
                for g in range(G):
                    turn(g)
                    if g + 1 < G:
                        scores(g + 1)
                    values(g)
                after(pe, ol_rdy, G * b + G)
                for i in range(2):
                    for g in range(G):
                        t = slice(i * P, (i + 1) * P)
                        last = three(j_ps[i][:], OH[:, g, t], OL[:, g, t], WOH[:, g, :], WOL[:, g, :], g == 0, g == G - 1)
                    last.then_inc(wo_done, 1)
                for i in range(2):
                    after(pe, xs_rdy, 2 * b + i + 1)
                    for c in range(KC):
                        last = nc.tensor.transpose(t_ps[i][:, c, :], xs[:, i, c * P:(c + 1) * P], ident[:])
                    last.then_inc(xt_done, 1)
            over_batches(pe, batch)


def cross(nc, splitter, A, ident, x2T, xtok):
    with ExitStack() as ctx:
        def sb(name, shape, dt=F32):
            return ctx.enter_context(nc.sbuf_tensor(name, shape, dt))

        def sem(name):
            return ctx.enter_context(nc.semaphore(name))

        WH = [sb(f"xW{n}H", [P, KC, D], F32R) for n in "qkv"]
        WL = [sb(f"xW{n}L", [P, KC, D], F32R) for n in "qkv"]
        WOH, WOL = sb("xWoH", [P, KC, D], F32R), sb("xWoL", [P, KC, D], F32R)
        splitter.split([(A["xw" + "qkv"[n]], WH[n][:], WL[n][:]) for n in range(3)] + [(A["xwo"], WOH[:], WOL[:])])
        bias = sb("bias", [P, 3, KC])
        bo = sb("bo_rows", [P, D])
        XH, XL = sb("xXH", [P, KC, S], F32R), sb("xXL", [P, KC, S], F32R)
        FM = [sb(f"fm{n}", [P, KC, S]) for n in "qkv"]
        cT = FM[0]
        QS, KS = sb("QS", [2 * HD, NH, S]), sb("KS", [ROWS, NH, S])
        QG = sb("QG", [ROWS, 2, 4, P])
        pr, PT = sb("pr", [P, 2, 4, P]), sb("xPT", [P, 2, 4, P])
        VG = sb("VG", [P, 2, 4, HD])
        mx, nm, sums, rinv = (sb("x" + n, [P, 2, 4]) for n in ("mx", "nm", "sums", "rinv"))
        r, xs = sb("xr", [P, 2, D]), sb("xxs", [P, 2, D])
        st, mv, ve, rstd, half = sb("xst", [P, 2, 6]), sb("xmv", [P, 2, 2]), sb("xve", [P, 2]), sb("xrstd", [P, 2]), sb("xhalf", [P, 2])
        s_ps, t_ps = ([ctx.enter_context(nc.psum_tensor(f"x{n}_ps{i}", [P, 4, P], F32)) for i in range(2)] for n in "st")
        o_ps, j_ps = ([ctx.enter_context(nc.psum_tensor(f"x{n}_ps{i}", [P, 512], F32)) for i in range(2)] for n in "oj")

        l_c, l_b, l_ks, l_qs, l_vs, onehot_in = (sem(n) for n in ("l_c", "l_b", "l_ks", "l_qs", "l_vs", "onehot_in"))
        consts, past = sem("x_consts"), sem("x_past")
        xh_rdy, xl_rdy = sem("x_xh"), sem("x_xl")
        proj_done, k_rdy, v_rdy, q_rdy = sem("x_proj"), sem("k_rdy"), sem("xv_rdy"), sem("q_rdy")
        qg_rdy, vg_rdy = sem("qg_rdy"), sem("vg_rdy")
        s_done, max_rdy, exp_done, rinv_rdy, norm_rdy = (sem("x_" + n) for n in ("s_done", "max_rdy", "exp_done", "rinv_rdy", "norm_rdy"))
        t_done, pt_rdy, o_done = sem("x_t_done"), sem("x_pt_rdy"), sem("x_o_done")
        r_rdy, wo_done, ve_rdy, rstd_rdy, xs_rdy, xt_done, xt_act, xt_dve, xtok_rdy = (
            sem("x_" + n) for n in ("r_rdy", "wo_done", "ve_rdy", "rstd_rdy", "xs_rdy", "xt_done", "xt_act", "xt_dve", "xtok_rdy"))
        dve_steps = sem("x_dve_steps")
        NPJ = 3 * KC
        block = ctx.enter_context(nc.Block())

        @block.sync
        def _(sp):
            sp.dma_start(bias[:], A["xb"]).then_inc(l_b, 16)
            sp.dma_start(bo[:], A["xbo"].partition_broadcast(P)).then_inc(l_b, 16)
            sp.wait_ge(consts, 6)
            sp.dma_start(QG[96:ROWS, :, :, :], QG[0:8, :, :, :]).then_inc(onehot_in, 16)
            sp.dma_start(KS[96:ROWS, :, :], KS[0:8, :, :]).then_inc(onehot_in, 16)
            sp.wait_ge(onehot_in, 32)

            def batch(b):
                after(sp, l_qs, 64 * b)
                sp.dma_start(cT[:], A["cT"][:, :, bass.ds(b * S, S)]).then_inc(l_c, 16)
                after(sp, s_done, NQ * b)
                for stack, rows, fm, ready, landed in ((KS, 0, FM[1], k_rdy, l_ks), (QS, 32, FM[2], v_rdy, l_vs),
                                                       (QS, 0, FM[0], q_rdy, l_qs)):
                    after(sp, ready, KC * (b + 1))
                    for j in range(4):
                        sp.dma_start(stack[rows:rows + HD, j:NH:4, :], fm[HD * j:HD * j + HD, :, :]).then_inc(landed, 16)
            over_batches(sp, batch)

        @block.gpsimd
        def _(pool):
            nc.gpsimd.memset(half[:], -0.5).then_inc(consts, 1)
            nc.gpsimd.memset(QG[:], 0.0).then_inc(consts, 1)
            nc.gpsimd.memset(KS[:], 0.0).then_inc(consts, 1)
            pool.wait_ge(consts, 3)
            nc.gpsimd.memset(KS[0:8, :, :], NEG).then_inc(consts, 1)
            pool.wait_ge(consts, 4)
            for part, fill in ((QG[0:8, :, :, :].rearrange("p s a (h t) -> p (s a h) t", t=8), 1.0),
                               (KS[0:8, :, :].rearrange("p h (a t) -> p (h a) t", t=8), 0.0)):
                nc.gpsimd.affine_select(out=part, in_=part, compare_op=ALU.not_equal, fill=fill, base=0,
                                        pattern=[[0, part.shape[1]], [1, 8]], channel_multiplier=-1).then_inc(consts, 1)
            pool.wait_ge(l_b, 32)

            def batch(b):
                after(pool, xs_rdy, 2 * b)
                alone(pool, past)
                nc.gpsimd.tensor_tensor(r[:, 0:1, :], xtok[:, bass.ds(2 * b, 1), :], bo[:].unsqueeze(1), ALU.add)
                nc.gpsimd.tensor_tensor(r[:, 1:2, :], xtok[:, bass.ds(2 * b + 1, 1), :], bo[:].unsqueeze(1), ALU.add).then_inc(r_rdy, 1)
                for q in range(NQ):
                    u = q % 2
                    after(pool, rinv_rdy, NQ * b + q + 1)
                    nc.gpsimd.tensor_tensor(pr[:, u, :, :], pr[:, u, :, :], rinv[:, u, :].unsqueeze(2).to_broadcast([P, 4, P]),
                                            ALU.mult).then_inc(norm_rdy, 1)
                for i in range(2):
                    after(pool, ve_rdy, 2 * b + i + 1)
                    nc.gpsimd.tensor_tensor(rstd[:, i:i + 1], ve[:, i:i + 1], half[:, i:i + 1], ALU.pow).then_inc(rstd_rdy, 1)
                for i in range(2):
                    after(pool, xs_rdy, 2 * b + i + 1)
                    alone(pool, past)
                    nc.gpsimd.tensor_copy(xtok[:, bass.ds(2 * b + i, 1), :], xs[:, i:i + 1, :]).then_inc(xtok_rdy, 1)
            over_batches(pool, batch)

        @block.scalar
        def _(act):
            copy = lambda out, src: nc.scalar.activation(out, src, ACT.Copy)
            act.wait_ge(l_b, 32)

            def batch(b):
                after(act, l_c, 16 * (b + 1))
                after(act, wo_done, 2 * b)
                copy(XH[:], cT[:]).then_inc(xh_rdy, 1)
                for c in range(KC):
                    after(act, proj_done, NPJ * b + KC + c + 1)
                    if c == 0:
                        after(act, l_vs, 64 * b)
                    nc.scalar.activation(FM[2][:, c, :], j_ps[c % 2][:, 0:S], ACT.Identity, bias=bias[:, 2, c:c + 1]).then_inc(v_rdy, 1)
                copy(XH[:], x2T[:, :, bass.ds(b * S, S)]).then_inc(xh_rdy, 1)
                for q in range(NQ):
                    u = q % 2
                    after(act, max_rdy, NQ * b + q + 1)
                    for a in range(4):
                        last = nc.scalar.activation(pr[:, u, a, :], s_ps[u][:, a, :], ACT.Exp,
                                                    bias=nm[:, u, a:a + 1], accum_out=sums[:, u, a:a + 1])
                    last.then_inc(exp_done, 1)
                    after(act, o_done, NQ * b + q - 1)
                    copy(VG[:, u, :, :].rearrange("p a d -> p (a d)"), j_ps[u][:, 0:P]).then_inc(vg_rdy, 1)
                for c in range(2):
                    after(act, o_done, NQ * b + (c + 1) * NQ // 2)
                    copy(XH[:, :, c * P:(c + 1) * P], o_ps[c][:].rearrange("p (i t) -> p i t", i=KC)).then_inc(xh_rdy, 1)
                for i in range(2):
                    after(act, xt_done, 2 * b + i + 1)
                    alone(act, past)
                    copy(x2T[:, 0:2, bass.ds(b * S + i * P, P)], t_ps[i][:, 0:2, :]).then_inc(xt_act, 1)
            over_batches(act, batch)

        @block.vector
        def _(dve):
            sub = lambda out, a, b: nc.vector.tensor_tensor(out, a, b, ALU.subtract)
            dve.wait_ge(l_b, 32)

            def batch(b):
                own = Steps(dve, dve_steps, NQ + 2 * 3, b)
                after(dve, xh_rdy, 4 * b + 1)
                sub(XL[:], cT[:], XH[:].bitcast(F32)).then_inc(xl_rdy, 1)
                after(dve, l_ks, 64 * b)
                for c in range(KC):
                    after(dve, proj_done, NPJ * b + c + 1)
                    nc.vector.tensor_scalar(FM[1][:, c, :], j_ps[c % 2][:, 0:S], bias[:, 1, c:c + 1], None, ALU.add).then_inc(k_rdy, 1)
                after(dve, xh_rdy, 4 * b + 2)
                sub(XL[:], x2T[:, :, bass.ds(b * S, S)], XH[:].bitcast(F32)).then_inc(xl_rdy, 1)
                after(dve, xl_rdy, 3 * b + 2)
                for c in range(KC):
                    after(dve, proj_done, NPJ * b + 2 * KC + c + 1)
                    nc.vector.tensor_scalar(FM[0][:, c, :], j_ps[c % 2][:, 0:S], bias[:, 0, c:c + 1], None, ALU.add).then_inc(q_rdy, 1)

                def group_queries(q):
                    u = q % 2
                    after(dve, s_done, NQ * b + q - 1)
                    nc.vector.tensor_copy(QG[0:2 * HD, u, :, :].rearrange("p a (h t) -> p a h t", t=8),
                                          QS[:, :, 32 * q:32 * q + 32].rearrange("p h (a t) -> p a h t", t=8)).then_inc(qg_rdy, 1)

                def maxima(q):
                    u = q % 2
                    after(dve, s_done, NQ * b + q + 1)
                    own.did(nc.vector.reduce_max(mx[:, u, :], s_ps[u][:], AX_X))
                    own.settle()
                    nc.vector.tensor_scalar(nm[:, u, :], mx[:, u, :], -1.0, None, ALU.mult).then_inc(max_rdy, 1)

                def sums_in(q):
                    u = q % 2
                    after(dve, exp_done, NQ * b + q + 1)
                    nc.vector.reciprocal(rinv[:, u, :], sums[:, u, :]).then_inc(rinv_rdy, 1)

                def pt_copy(q):
                    after(dve, t_done, NQ * b + q + 1)
                    nc.vector.tensor_copy(PT[:, q % 2, :, :], t_ps[q % 2][:]).then_inc(pt_rdy, 1)

                after(dve, l_vs, 64 * (b + 1))
                after(dve, l_qs, 64 * (b + 1))
                group_queries(0)
                group_queries(1)
                for q in range(2):
                    maxima(q)
                    group_queries(q + 2)
                for q in range(NQ):
                    sums_in(q)
                    if q + 2 < NQ:
                        maxima(q + 2)
                    if q + 4 < NQ:
                        group_queries(q + 4)
                    pt_copy(q)
                for c in range(2):
                    after(dve, xh_rdy, 4 * b + 3 + c)
                    last = sub(XL[:, :, c * P:(c + 1) * P], o_ps[c][:].rearrange("p (i t) -> p i t", i=KC),
                               XH[:, :, c * P:(c + 1) * P].bitcast(F32))
                last.then_inc(xl_rdy, 1)
                after(dve, r_rdy, b + 1)
                for i in range(2):
                    after(dve, wo_done, 2 * b + i + 1)
                    own.did(nc.vector.tensor_tensor(r[:, i, :], j_ps[i][:], r[:, i, :], ALU.add))
                    own.settle()
                    own.did(nc.vector.bn_stats(st[:, i, :], r[:, i, :]))
                    own.settle()
                    alone(dve, past)
                    own.did(nc.vector.bn_aggr(mv[:, i, :], st[:, i, :]))
                    own.settle()
                    nc.vector.tensor_scalar(ve[:, i:i + 1], mv[:, i, 1:2], EPS, None, ALU.add).then_inc(ve_rdy, 1)
                for i in range(2):
                    after(dve, rstd_rdy, 2 * b + i + 1)
                    after(dve, xtok_rdy, 2 * b)
                    after(dve, xt_done, 2 * b)
                    nc.vector.tensor_scalar(xs[:, i, :], r[:, i, :], mv[:, i, 0:1], rstd[:, i:i + 1],
                                            ALU.subtract, ALU.mult).then_inc(xs_rdy, 1)
                for i in range(2):
                    after(dve, xt_act, 2 * b + i + 1)
                    alone(dve, past)
                    nc.vector.tensor_copy(x2T[:, 2:4, bass.ds(b * S + i * P, P)], t_ps[i][:, 2:4, :]).then_inc(xt_dve, 1)
                own.close()
            over_batches(dve, batch)

        @block.tensor
        def _(pe):
            mm = nc.tensor.matmul

            def three(out, wh, wl, xh, xl, first, last):
                mm(out, wh, xh, start=first, stop=False)
                mm(out, wh, xl, start=False, stop=False)
                return mm(out, wl, xh, start=False, stop=last)

            pe.wait_ge(onehot_in, 32)

            def batch(b):
                after(pe, ve_rdy, 2 * b)

                def project(n, rank):
                    for c in range(KC):
                        at = rank * KC + c
                        if at == KC + 1 or at == KC:
                            after(pe, k_rdy, KC * b + at - 1)
                        elif at > KC + 1 and at < 2 * KC + 2:
                            after(pe, v_rdy, KC * b + at - 1 - KC)
                        elif at >= 2:
                            after(pe, k_rdy if rank == 0 else q_rdy, KC * b + c - 1)
                        cols = slice(c * P, (c + 1) * P)
                        for k in range(KC):
                            last = three(j_ps[c % 2][:, 0:S], WH[n][:, k, cols], WL[n][:, k, cols], XH[:, k, :], XL[:, k, :],
                                         k == 0, k == KC - 1)
                        last.then_inc(proj_done, 1)

                after(pe, xl_rdy, 3 * b + 1)
                project(1, 0)
                project(2, 1)
                after(pe, xl_rdy, 3 * b + 2)
                project(0, 2)
                after(pe, q_rdy, KC * (b + 1))
                after(pe, l_ks, 64 * (b + 1))

                def scores(q):
                    after(pe, qg_rdy, NQ * b + q + 1)
                    if q >= 2:
                        after(pe, exp_done, NQ * b + q - 1)
                    if q >= 2:
                        after(pe, vg_rdy, NQ * b + q - 1)
                    for a in range(4):
                        t = slice((4 * q + a) * 8, (4 * q + a) * 8 + 8)
                        mm(s_ps[q % 2][:, a, :], QG[:, q % 2, a, :], KS[:, :, t], start=True, stop=True)
                    for a in range(4):
                        last = nc.tensor.transpose(j_ps[q % 2][:, a * HD:(a + 1) * HD], QG[32:64, q % 2, a, :], ident[32:64, 32:64])
                    last.then_inc(s_done, 1)

                def turn(q):
                    after(pe, norm_rdy, NQ * b + q + 1)
                    if q >= 2:
                        after(pe, pt_rdy, NQ * b + q - 1)
                    for a in range(4):
                        last = nc.tensor.transpose(t_ps[q % 2][:, a, :], pr[:, q % 2, a, :], ident[:])
                    last.then_inc(t_done, 1)

                def values(q):
                    after(pe, pt_rdy, NQ * b + q + 1)
                    after(pe, vg_rdy, NQ * b + q + 1)
                    half_of = q // (NQ // 2)
                    out = o_ps[half_of][:].rearrange("p (i t) -> p i t", i=KC)
                    for a in range(4):
                        group = 4 * q + a
                        t = slice(group * 8 % P, group * 8 % P + 8)
                        probs = PT[:, q % 2, a, :].rearrange("p (i j t) -> p i j t", i=4, j=4)
                        for j in range(4):
                            last = mm(out[HD * j:HD * j + HD, :, t], VG[:, q % 2, a, :], probs[:, :, j, :], start=True, stop=True)
                    last.then_inc(o_done, 1)

                scores(0)
                scores(1)
                for q in range(NQ):
                    if q >= 1:
                        values(q - 1)
                    turn(q)
                    if q + 2 < NQ:
                        scores(q + 2)
                values(NQ - 1)
                after(pe, xl_rdy, 3 * b + 3)
                after(pe, vg_rdy, NQ * (b + 1))
                for i in range(2):
                    t = slice(i * P, (i + 1) * P)
                    for k in range(KC):
                        last = three(j_ps[i][:], XH[:, k, t], XL[:, k, t], WOH[:, k, :], WOL[:, k, :], k == 0, k == KC - 1)
                    last.then_inc(wo_done, 1)
                for i in range(2):
                    after(pe, xs_rdy, 2 * b + i + 1)
                    for c in range(KC):
                        last = nc.tensor.transpose(t_ps[i][:, c, :], xs[:, i, c * P:(c + 1) * P], ident[:])
                    last.then_inc(xt_done, 1)
                after(pe, xt_dve, 2 * (b + 1))
            over_batches(pe, batch)


def gating(nc, splitter, A, ident, x2T, scal, soft_f, soft_hl):
    with ExitStack() as ctx:
        def sb(name, shape, dt=F32):
            return ctx.enter_context(nc.sbuf_tensor(name, shape, dt))

        def sem(name):
            return ctx.enter_context(nc.semaphore(name))

        GH, GL = sb("GH", [P, KC, E], F32R), sb("GL", [P, KC, E], F32R)
        splitter.split([(A["gate"], GH[:], GL[:])])
        XH, XL = sb("gXH", [P, 2, KC, TB], F32R), sb("gXL", [P, 2, KC, TB], F32R)
        lgT = sb("lgT", [E, T])
        sc, ex, wd, flat = (sb(n, [P, NT, E]) for n in ("sc", "ex", "wd", "flat"))
        ext = sb("ext", [P, NT, E + 2])
        rest = sb("rest", [P, NT, E + 2])
        top = sb("top", [P, NT, 8])
        col, col2 = sb("col", [P, NT, F]), sb("col2", [P, NT, F])
        wdT, softT, soft_h, soft_l = sb("wdT", [E, T]), sb("softT", [E, T]), sb("soft_h", [E, T], F32R), sb("soft_l", [E, T], F32R)
        inv_i, inv_f, neg, row, sel = sb("inv_i", [E, E], mybir.dt.int32), sb("inv_f", [E, E]), sb("neg", [E, E]), sb("row", [E, 1]), sb("sel", [E, E])
        row_i = sb("row_i", [E, 1], mybir.dt.int32)
        lg_ps = [ctx.enter_context(nc.psum_tensor(f"lg_ps{i}", [P, TB], F32)) for i in range(2)]
        tok_ps = [ctx.enter_context(nc.psum_tensor(f"tok_ps{i}", [P, 8, E], F32)) for i in range(2)]
        tr_ps = [ctx.enter_context(nc.psum_tensor(f"tr_ps{i}", [P, TB], F32)) for i in range(2)]

        l_inv, stored, iota_in = sem("l_inv"), sem("stored"), sem("iota_in")
        xh_rdy, xl_rdy, lg_done, lg_rdy, tok_done = (sem("g_" + n) for n in ("xh", "xl", "lg_done", "lg_rdy", "tok_done"))
        ex_rdy, soft_e, steps, wd_rdy, wdT_done, wdT_rdy, flat_done, z_rdy, z_exp, soft_rdy, sT_done, sT_rdy, h_rdy, l_rdy = (
            sem("g_" + n) for n in ("ex_rdy", "soft_e", "steps", "wd_rdy", "wdT_done", "wdT_rdy", "flat_done", "z_rdy", "z_exp",
                                    "soft_rdy", "sT_done", "sT_rdy", "h_rdy", "l_rdy"))
        block = ctx.enter_context(nc.Block())

        @block.sync
        def _(sp):
            sp.dma_start(inv_i[:], A["inv"].partition_broadcast(E)).then_inc(l_inv, 16)
            sp.wait_ge(sT_rdy, NB)
            sp.dma_start(soft_f.rearrange("f k t -> (f k) t"), softT[:]).then_inc(stored, 16)
            sp.wait_ge(h_rdy, 1)
            sp.dma_start(soft_hl[0].rearrange("f k t -> (f k) t"), soft_h[:].bitcast(F32)).then_inc(stored, 16)
            sp.wait_ge(l_rdy, 1)
            sp.dma_start(soft_hl[1].rearrange("f k t -> (f k) t"), soft_l[:].bitcast(F32)).then_inc(stored, 16)
            sp.wait_ge(stored, 48)

        @block.gpsimd
        def _(pool):
            nc.gpsimd.iota(row_i[:], pattern=[[0, 1]], base=0, channel_multiplier=1).then_inc(iota_in, 1)

        @block.scalar
        def _(act):
            copy = lambda out, src: nc.scalar.activation(out, src, ACT.Copy)
            for tb in range(NB):
                after(act, lg_done, tb - 1)
                copy(XH[:, tb % 2, :, :], x2T[:, :, tb * TB:(tb + 1) * TB]).then_inc(xh_rdy, 1)
                if tb >= 1:
                    act.wait_ge(lg_done, tb)
                    copy(lgT[:, (tb - 1) * TB:tb * TB], lg_ps[(tb - 1) % 2][0:E, :]).then_inc(lg_rdy, 1)
            act.wait_ge(lg_done, NB)
            copy(lgT[:, (NB - 1) * TB:NB * TB], lg_ps[(NB - 1) % 2][0:E, :]).then_inc(lg_rdy, 1)
            act.wait_ge(ex_rdy, 1)
            nc.scalar.activation(ex[:], ex[:], ACT.Exp).then_inc(soft_e, 1)
            for n in range(NB):
                act.wait_ge(wdT_done, n + 1)
                copy(wdT[:, n * TB:(n + 1) * TB], tr_ps[n % 2][0:E, :]).then_inc(wdT_rdy, 1)
            act.wait_ge(z_rdy, 1)
            nc.scalar.activation(ex[:], ex[:], ACT.Exp).then_inc(z_exp, 1)
            for n in range(NB):
                act.wait_ge(sT_done, n + 1)
                copy(softT[:, n * TB:(n + 1) * TB], tr_ps[n % 2][0:E, :]).then_inc(sT_rdy, 1)
            act.wait_ge(sT_rdy, NB)
            copy(soft_h[:], softT[:]).then_inc(h_rdy, 1)

        @block.vector
        def _(dve):
            sub = lambda out, a, b: nc.vector.tensor_tensor(out, a, b, ALU.subtract)
            own = Steps(dve, steps, 0, 0)

            def do(instruction):
                own.did(instruction)
                own.settle()

            for tb in range(NB):
                dve.wait_ge(xh_rdy, tb + 1)
                sub(XL[:, tb % 2, :, :], x2T[:, :, tb * TB:(tb + 1) * TB], XH[:, tb % 2, :, :].bitcast(F32)).then_inc(xl_rdy, 1)
            dve.wait_ge(l_inv, 16)
            dve.wait_ge(iota_in, 1)
            own.did(nc.vector.tensor_copy(row[:], row_i[:]))
            do(nc.vector.tensor_copy(inv_f[:], inv_i[:]))
            do(nc.vector.tensor_scalar(neg[:], inv_f[:], 0.0, float(E), ALU.is_lt, ALU.mult))
            do(nc.vector.tensor_tensor(inv_f[:], inv_f[:], neg[:], ALU.add))
            do(nc.vector.tensor_scalar(sel[:], inv_f[:], row[:, 0:1], None, ALU.is_equal))
            do(nc.vector.memset(ext[:, :, E:E + 2], -1.0))

            dve.wait_ge(tok_done, 2)
            for i in range(2):
                last = nc.vector.tensor_copy(sc[:, 8 * i:8 * i + 8, :], tok_ps[i][:])
            do(last)
            do(nc.vector.reduce_max(col[:, :, 0:1], sc[:], AX_X))
            sub(ex[:], sc[:], col[:, :, 0:1].to_broadcast([P, NT, E])).then_inc(ex_rdy, 1)
            dve.wait_ge(soft_e, 1)
            do(nc.vector.reduce_sum(col[:, :, 0:1], ex[:], AX_X))
            do(nc.vector.reciprocal(col[:, :, 0:1], col[:, :, 0:1]))
            do(nc.vector.tensor_tensor(sc[:], ex[:], col[:, :, 0:1].to_broadcast([P, NT, E]), ALU.mult))
            do(nc.vector.tensor_copy(ext[:, :, 0:E], sc[:]))
            for i in range(NT):
                last = nc.vector.max(top[:, i, :], ext[:, i, 0:E])
            do(last)
            do(nc.vector.memset(top[:, :, TOPK:8], -1.0))
            for i in range(NT):
                last = nc.vector.match_replace(rest[:, i, :], top[:, i, :], ext[:, i, :], 0.0)
            do(last)
            sub(wd[:], sc[:], rest[:, :, 0:E]).then_inc(wd_rdy, 1)
            dve.wait_ge(flat_done, 2)
            for i in range(2):
                last = nc.vector.tensor_copy(flat[:, 8 * i:8 * i + 8, :], tok_ps[i][:])
            do(last)
            by_expert = lambda t: t[:].rearrange("p n (f k) -> p n f k", k=K8)
            do(nc.vector.tensor_reduce(scal[:], by_expert(flat), axis=AX_X, op=ALU.add))
            do(nc.vector.tensor_scalar(ex[:], flat[:], 0.0, -1e9, ALU.is_equal, ALU.mult))
            do(nc.vector.tensor_tensor(ex[:], ex[:], flat[:], ALU.add))
            do(nc.vector.tensor_reduce(col[:], by_expert(ex), axis=AX_X, op=ALU.max))
            cols = lambda c: c[:].unsqueeze(3).to_broadcast([P, NT, F, K8])
            sub(by_expert(ex), by_expert(ex), cols(col)).then_inc(z_rdy, 1)
            dve.wait_ge(z_exp, 1)
            do(nc.vector.tensor_reduce(col2[:], by_expert(ex), axis=AX_X, op=ALU.add))
            do(nc.vector.reciprocal(col2[:], col2[:]))
            nc.vector.tensor_tensor(by_expert(wd), by_expert(ex), cols(col2), ALU.mult).then_inc(soft_rdy, 1)
            dve.wait_ge(h_rdy, 1)
            sub(soft_l[:], softT[:], soft_h[:].bitcast(F32)).then_inc(l_rdy, 1)

        @block.tensor
        def _(pe):
            mm = nc.tensor.matmul
            for tb in range(NB):
                pe.wait_ge(xl_rdy, tb + 1)
                if tb >= 2:
                    pe.wait_ge(lg_rdy, tb - 1)
                for k in range(KC):
                    for n, (w, x) in enumerate(((GH, XH), (GH, XL), (GL, XH), (GL, XL))):
                        last = mm(lg_ps[tb % 2][0:E, :], w[:, k, :], x[:, tb % 2, k, :], start=(k == 0 and n == 0),
                                  stop=(k == KC - 1 and n == 3))
                last.then_inc(lg_done, 1)
            for i in range(NT):
                if i % 4 == 0:
                    pe.wait_ge(lg_rdy, i // 4 + 1)
                last = nc.tensor.transpose(tok_ps[i // 8][:, i % 8, :], lgT[:, i * P:(i + 1) * P], ident[0:E, 0:E])
                if i % 8 == 7:
                    last.then_inc(tok_done, 1)

            def to_rows(done, copied):
                for i in range(NT):
                    if i % 4 == 0 and i >= 8:
                        pe.wait_ge(copied, i // 4 - 1)
                    last = nc.tensor.transpose(tr_ps[i // 4 % 2][0:E, i % 4 * P:(i % 4 + 1) * P], wd[:, i, :], ident[:])
                    if i % 4 == 3:
                        last.then_inc(done, 1)

            pe.wait_ge(wd_rdy, 1)
            to_rows(wdT_done, wdT_rdy)
            for i in range(NT):
                if i % 4 == 0:
                    pe.wait_ge(wdT_rdy, i // 4 + 1)
                last = mm(tok_ps[i // 8][:, i % 8, :], wdT[:, i * P:(i + 1) * P], sel[:], start=True, stop=True)
                if i % 8 == 7:
                    last.then_inc(flat_done, 1)
            pe.wait_ge(soft_rdy, 1)
            to_rows(sT_done, sT_rdy)


def experts(nc, A, x2T, xtok, scal, soft_f, soft_hl):
    F32, F32R = mybir.dt.float32, mybir.dt.float32r
    with ExitStack() as ctx:
        def sb(name, shape, dt=F32):
            return ctx.enter_context(nc.sbuf_tensor(name, shape, dt))

        def sem(name):
            return ctx.enter_context(nc.semaphore(name))

        MUS = sb("MUS", [72, D], F32R)
        QAH, QAL = sb("QAH", [P, KC, P], F32R), sb("QAL", [P, KC, P], F32R)
        GUH = [sb(f"GUH{j}", [P, KC, 2, M], F32R) for j, M in enumerate(ITILES)]
        GUL = [sb(f"GUL{j}", [P, KC, 2, M], F32R) for j, M in enumerate(ITILES)]
        QBH, QBL = sb("QBH", [P, 2, I], F32R), sb("QBL", [P, I], F32R)
        QDH, QDL = sb("QDH", [P, NI, KR], F32R), sb("QDL", [P, NI, KR], F32R)
        DWH, DWL = sb("DWH", [P, NI, D], F32R), sb("DWL", [P, NI, D], F32R)
        DBH, DBL = sb("DBH", [P, D], F32R), sb("DBL", [KR, D], F32R)
        mu_raw, qa_raw = sb("mu_raw", [72, D]), sb("qa_raw", [P, KC, P])
        gu_raw = [sb(f"gu_raw{j}", [P, KC, 2, M]) for j, M in enumerate(ITILES)]
        qb_raw, qb_scale = sb("qb_raw", [P, 2, I]), sb("qb_scale", [P, 2, I])
        qd_raw, dw_raw = sb("qd_raw", [P, NI, KR]), sb("dw_raw", [P, NI, D])
        db_raw, db_scale = sb("db_raw", [P, D]), sb("db_scale", [P, D])
        XH, XL = sb("XH", [P, KC, TB], F32R), sb("XL", [P, KC, TB], F32R)
        xe = sb("xe", [P, 2, TB])
        HH, HL = sb("HH", [P, NI, TB], F32R), sb("HL", [P, NI, TB], F32R)
        h = sb("h", [P, 2, TB])
        sg = sb("sg", [P, 2, TB])
        low = sb("low", [P, TB])
        G2, U2, D2 = sb("G2", [P, TB], F32R), sb("U2", [P, TB], F32R), sb("D2", [P, TB], F32R)
        wrep = sb("wrep", [P, 2, TB])
        ws = sb("ws", [72, 2, TB], F32R)
        sf = sb("sf", [P, NT])

        pair = [[ctx.enter_context(nc.psum_tensor(f"pair{b}{s}", [P, TB], F32)) for s in range(2)] for b in range(2)]
        qa_ps = ctx.enter_context(nc.psum_tensor("qa_ps", [P, TB], F32))
        qd_ps = ctx.enter_context(nc.psum_tensor("qd_ps", [P, TB], F32))
        y_ps = [ctx.enter_context(nc.psum_tensor(f"y_ps{b}", [P, D], F32)) for b in range(2)]

        l_gu = [sem(f"l_gu{j}") for j in range(NI)]
        l_dw, l_mu, l_qa, l_qb, l_qd, l_db = (sem(n) for n in ("l_dw", "l_mu", "l_qa", "l_qb", "l_qd", "l_db"))
        l_wrep, l_ws = [sem(f"l_wrep{b}") for b in range(2)], [sem(f"l_ws{b}") for b in range(2)]
        qb_scaled, db_scaled = sem("qb_scaled"), sem("db_scaled")
        gu_hi, dw_hi, lr_hi = sem("gu_hi"), sem("dw_hi"), sem("lr_hi")
        w_gu, w_dw, w_mu, w_qa, w_qb, w_qd, w_db = (sem(n) for n in ("w_gu", "w_dw", "w_mu", "w_qa", "w_qb", "w_qd", "w_db"))
        zeroed = sem("zeroed")
        xe_done, qa_done, gu_done, qd_done, y_done = (sem(n) for n in ("xe_done", "qa_done", "gu_done", "qd_done", "y_done"))
        xe_rdy, xh_rdy, xl_rdy = sem("xe_rdy"), sem("xh_rdy"), sem("xl_rdy")
        low_rdy, gu2_hi, gu2_rdy, d2_hi, d2_rdy = (sem(n) for n in ("low_rdy", "gu2_hi", "gu2_rdy", "d2_hi", "d2_rdy"))
        lowd_rdy = sem("lowd_rdy")
        silu_rdy, h_rdy, hh_rdy, hl_rdy, y_added, sf_rdy = (sem(n) for n in ("silu_rdy", "h_rdy", "hh_rdy", "hl_rdy", "y_added", "sf_rdy"))
        block = ctx.enter_context(nc.Block())

        def over_experts(eng, body):
            body(0, False, False)
            body(1, False, True)
            body(2, True, True)
            with eng.Fori(3, 1 + NF) as e:
                body(e, True, True)
            body(1 + NF, True, None)

        def slot(tb, j):
            return (NI * tb + j) % 2

        @block.sync
        def _(sp):
            def load(e, routed):
                f = e - 2
                at = 0
                for j, M in enumerate(ITILES):
                    after(sp, w_gu, NI * (e - 1) + j + 1)
                    sp.dma_start(gu_raw[j][:].rearrange("p k s m -> p (k s m)"),
                                 A["gu"][e, :, at:at + KC * 2 * M]).then_inc(l_gu[j], 16)
                    at += KC * 2 * M
                after(sp, w_dw, e)
                sp.dma_start(dw_raw[:, 0:NI - 1, :], A["dw"][e, 0:(NI - 1) * P, :].rearrange("(j p) n -> p j n", p=P)).then_inc(l_dw, 16)
                sp.dma_start(dw_raw[0:ITILES[-1], NI - 1, :], A["dw"][e, (NI - 1) * P:I, :]).then_inc(l_dw, 16)
                if not routed:
                    return
                after(sp, w_mu, f)
                sp.wait_ge(zeroed, 1)
                for r in (0, 32, 64):
                    sp.dma_start(mu_raw[r:r + K8, :], A["mu"][f, :, :]).then_inc(l_mu, 16)
                after(sp, w_qa, f)
                sp.dma_start(qa_raw[:].rearrange("p k m -> p (k m)"), A["qa"][f, :, :]).then_inc(l_qa, 16)
                after(sp, w_qb, f)
                for r in (0, KR):
                    sp.dma_start(qb_raw[r:r + KR, :, :], A["qb"][f, :, :, :]).then_inc(l_qb, 16)
                sp.dma_start(qb_scale[:].rearrange("p s i -> p (s i)"),
                             A["gu_scale"][f, :].partition_broadcast(P)).then_inc(l_qb, 16)
                after(sp, w_qd, f)
                sp.dma_start(qd_raw[:, 0:NI - 1, :], A["qd"][f, 0:(NI - 1) * P, :].rearrange("(j p) n -> p j n", p=P)).then_inc(l_qd, 16)
                sp.dma_start(qd_raw[0:ITILES[-1], NI - 1, :], A["qd"][f, (NI - 1) * P:I, :]).then_inc(l_qd, 16)
                after(sp, w_db, f)
                for r in (0, KR):
                    sp.dma_start(db_raw[r:r + KR, :], A["db"][f, :, :]).then_inc(l_db, 16)
                sp.dma_start(db_scale[:], A["d_scale"][f, :].partition_broadcast(P)).then_inc(l_db, 16)

            def load_ws(f, tb):
                n = f * NB + tb
                b = tb % 2
                sp.wait_ge(zeroed, 2)
                after(sp, xe_done, KC * (n - 1))
                for r, part in ((0, 0), (32, 1), (64, 0)):
                    sp.dma_start(ws[r:r + K8, b, :].bitcast(F32),
                                 soft_hl[part, f, :, tb * TB:(tb + 1) * TB]).then_inc(l_ws[b], 16)

            def load_wrep(f, tb):
                n = f * NB + tb
                b = tb % 2
                after(sp, lowd_rdy, n - 1)
                for s in range(2):
                    sp.dma_start(wrep[s * KR:(s + 1) * KR, b, :],
                                 soft_f[f, :, tb * TB:(tb + 1) * TB].unsqueeze(1).to_broadcast([K8, R8, TB])).then_inc(l_wrep[b], 16)

            load(0, False)

            def body(e, routed, nxt):
                f = e - 2
                for tb in range(NB):
                    if (routed and tb < NB - 1) or (nxt and tb == NB - 1):
                        load_wrep(f + (tb + 1) // NB, (tb + 1) % NB)
                    if (routed and tb < NB - 2) or (nxt and tb >= NB - 2):
                        load_ws(f + (tb + 2) // NB, (tb + 2) % NB)
                    if tb == 0 and nxt is not None:
                        load(e + 1, nxt)
            over_experts(sp, body)

        @block.gpsimd
        def _(pool):
            nc.gpsimd.memset(mu_raw[:], 0.0).then_inc(zeroed, 1)
            nc.gpsimd.memset(ws[:].bitcast(F32), 0.0).then_inc(zeroed, 1)
            pool.wait_ge(zeroed, 2)

            def body(e, routed, nxt):
                f = e - 2
                for tb in range(NB):
                    if nxt and tb == NB - 2:
                        pool.wait_ge(l_qb, 48 * (f + 2))
                        nc.gpsimd.tensor_tensor(qb_raw[:], qb_raw[:], qb_scale[:], ALU.mult).then_inc(qb_scaled, 1)
                        pool.wait_ge(l_db, 48 * (f + 2))
                        nc.gpsimd.tensor_tensor(db_raw[:], db_raw[:], db_scale[:], ALU.mult).then_inc(db_scaled, 1)
            over_experts(pool, body)

        @block.scalar
        def _(act):
            copy = lambda out, src: nc.scalar.activation(out, src, ACT.Copy)

            def gu_split(e, j):
                act.wait_ge(l_gu[j], 16 * (e + 1))
                after(act, gu_done, NI * NB * (e - 1) + NI * (NB - 1) + j + 1)
                copy(GUH[j][:], gu_raw[j][:]).then_inc(gu_hi, 1)

            def dw_split(e):
                act.wait_ge(l_dw, 32 * (e + 1))
                after(act, y_done, NB * 4 * e)
                copy(DWH[:, 0:NI - 1, :], dw_raw[:, 0:NI - 1, :])
                copy(DWH[0:ITILES[-1], NI - 1, :], dw_raw[0:ITILES[-1], NI - 1, :]).then_inc(dw_hi, 1)

            gu_split(0, 0), gu_split(0, 1), gu_split(0, 2), dw_split(0)
            for k in range(KC):
                copy(XH[:, k, :], x2T[:, k, 0:TB]).then_inc(xh_rdy, 1)

            def body(e, routed, nxt):
                f = e - 2
                for tb in range(NB):
                    s, n = e * NB + tb, f * NB + tb
                    turn = tb == NB - 1 and nxt is not None
                    if turn and nxt:
                        act.wait_ge(l_mu, 48 * (f + 2))
                        after(act, xe_done, KC * (n + 1))
                        copy(MUS[:], mu_raw[:]).then_inc(lr_hi, 1)
                    if routed:
                        act.wait_ge(low_rdy, n + 1)
                        copy(G2[0:KR, :], low[0:KR, :]).then_inc(gu2_hi, 1)
                        copy(U2[KR:P, :], low[KR:P, :]).then_inc(gu2_hi, 1)
                    if turn and nxt:
                        act.wait_ge(l_qa, 16 * (f + 2))
                        after(act, qa_done, n + 1)
                        copy(QAH[:], qa_raw[:]).then_inc(lr_hi, 1)
                    for j, M in enumerate(ITILES):
                        b = slot(tb, j)
                        act.wait_ge(gu_done, NI * s + j + 1)
                        nc.scalar.activation(sg[0:M, b, :], pair[b][0][0:M, :], ACT.Silu).then_inc(silu_rdy, 1)
                        act.wait_ge(h_rdy, NI * s + j + 1)
                        copy(HH[0:M, j, :], h[0:M, b, :]).then_inc(hh_rdy, 1)
                        if turn:
                            gu_split(e + 1, j)
                    if turn and nxt:
                        act.wait_ge(qb_scaled, f + 2)
                        copy(QBH[:], qb_raw[:]).then_inc(lr_hi, 1)

                    def next_x(k):
                        m = f * NB + tb + 1
                        if routed or turn and nxt:
                            act.wait_ge(xe_rdy, KC * m + k + 1)
                            copy(XH[:, k, :], xe[:, k % 2, :]).then_inc(xh_rdy, 1)
                        else:
                            t = (tb + 1) % NB * TB
                            copy(XH[:, k, :], x2T[:, k, t:t + TB]).then_inc(xh_rdy, 1)
                    more = tb < NB - 1 or nxt is not None
                    if more:
                        next_x(0), next_x(1)
                    if routed:
                        act.wait_ge(lowd_rdy, n + 1)
                        copy(D2[0:KR, :], low[0:KR, :]).then_inc(d2_hi, 1)
                    if turn and nxt:
                        act.wait_ge(l_qd, 32 * (f + 2))
                        after(act, qd_done, n + 1)
                        copy(QDH[:, 0:NI - 1, :], qd_raw[:, 0:NI - 1, :])
                        copy(QDH[0:ITILES[-1], NI - 1, :], qd_raw[0:ITILES[-1], NI - 1, :]).then_inc(lr_hi, 1)
                    if more:
                        next_x(2), next_x(3)
                    if turn:
                        dw_split(e + 1)
                        if nxt:
                            act.wait_ge(db_scaled, f + 2)
                            copy(DBH[:], db_raw[:]).then_inc(lr_hi, 1)
            over_experts(act, body)

        @block.vector
        def _(dve):
            sub = lambda out, a, b: nc.vector.tensor_tensor(out, a, b, ALU.subtract)

            def gu_split(e, j):
                dve.wait_ge(gu_hi, NI * e + j + 1)
                sub(GUL[j][:], gu_raw[j][:], GUH[j][:].bitcast(F32)).then_inc(w_gu, 1)

            def dw_split(e):
                dve.wait_ge(dw_hi, e + 1)
                sub(DWL[:, 0:NI - 1, :], dw_raw[:, 0:NI - 1, :], DWH[:, 0:NI - 1, :].bitcast(F32))
                M = ITILES[-1]
                sub(DWL[0:M, NI - 1, :], dw_raw[0:M, NI - 1, :], DWH[0:M, NI - 1, :].bitcast(F32)).then_inc(w_dw, 1)

            gu_split(0, 0), gu_split(0, 1), gu_split(0, 2), dw_split(0)
            for k in range(KC):
                dve.wait_ge(xh_rdy, k + 1)
                sub(XL[:, k, :], x2T[:, k, 0:TB], XH[:, k, :].bitcast(F32)).then_inc(xl_rdy, 1)

            def body(e, routed, nxt):
                f = e - 2
                if routed:
                    dve.wait_ge(y_added, 4 * NB * e)
                    nc.vector.tensor_copy(sf[:].unsqueeze(2), scal[:, :, bass.ds(f, 1)]).then_inc(sf_rdy, 1)
                for tb in range(NB):
                    s, n = e * NB + tb, f * NB + tb
                    turn = tb == NB - 1 and nxt is not None
                    hi = 5 * (f + 1)
                    if turn and nxt:
                        dve.wait_ge(lr_hi, hi + 1)
                        sub(MUS[64:72, :], mu_raw[64:72, :], MUS[64:72, :].bitcast(F32)).then_inc(w_mu, 1)
                    if routed:
                        dve.wait_ge(qa_done, n + 1)
                        dve.wait_ge(l_wrep[tb % 2], 32 * (2 * f + tb // 2 + 1))
                        after(dve, d2_rdy, n)
                        nc.vector.tensor_tensor(low[:], qa_ps[:], wrep[:, tb % 2, :], ALU.mult).then_inc(low_rdy, 1)
                        dve.wait_ge(gu2_hi, 2 * n + 1)
                        sub(G2[KR:P, :], low[0:KR, :], G2[0:KR, :].bitcast(F32)).then_inc(gu2_rdy, 1)
                        dve.wait_ge(gu2_hi, 2 * n + 2)
                        sub(U2[0:KR, :], low[KR:P, :], U2[KR:P, :].bitcast(F32)).then_inc(gu2_rdy, 1)
                    if turn and nxt:
                        dve.wait_ge(lr_hi, hi + 2)
                        sub(QAL[:], qa_raw[:], QAH[:].bitcast(F32)).then_inc(w_qa, 1)
                    for j, M in enumerate(ITILES):
                        b = slot(tb, j)
                        dve.wait_ge(silu_rdy, NI * s + j + 1)
                        nc.vector.tensor_tensor(h[0:M, b, :], pair[b][1][0:M, :], sg[0:M, b, :], ALU.mult).then_inc(h_rdy, 1)
                        dve.wait_ge(hh_rdy, NI * s + j + 1)
                        sub(HL[0:M, j, :], h[0:M, b, :], HH[0:M, j, :].bitcast(F32)).then_inc(hl_rdy, 1)
                        if turn:
                            gu_split(e + 1, j)
                    if turn and nxt:
                        dve.wait_ge(lr_hi, hi + 3)
                        sub(QBL[0:KR, :], qb_raw[0:KR, 0, :], QBH[0:KR, 0, :].bitcast(F32))
                        sub(QBL[KR:P, :], qb_raw[KR:P, 1, :], QBH[KR:P, 1, :].bitcast(F32)).then_inc(w_qb, 1)

                    m, sm = n + 1, s + 1
                    t = (tb + 1) % NB * TB
                    more = tb < NB - 1 or nxt is not None

                    def next_x(ks):
                        mixed = routed or turn and nxt
                        if mixed:
                            for k in ks:
                                dve.wait_ge(xe_done, KC * m + k + 1)
                                after(dve, xl_rdy, KC * sm + k - 1)
                                nc.vector.tensor_tensor(xe[:, k % 2, :], pair[slot(tb, 1 + k // 2)][k % 2][:],
                                                        x2T[:, k, t:t + TB], ALU.add).then_inc(xe_rdy, 1)
                        for k in ks:
                            dve.wait_ge(xh_rdy, KC * sm + k + 1)
                            src = xe[:, k % 2, :] if mixed else x2T[:, k, t:t + TB]
                            sub(XL[:, k, :], src, XH[:, k, :].bitcast(F32)).then_inc(xl_rdy, 1)
                    if more:
                        next_x((0, 1))
                    if routed:
                        dve.wait_ge(qd_done, n + 1)
                        dve.wait_ge(gu2_rdy, 2 * n + 2)
                        nc.vector.tensor_tensor(low[0:KR, :], qd_ps[0:KR, :], wrep[0:KR, tb % 2, :], ALU.mult).then_inc(lowd_rdy, 1)
                        dve.wait_ge(d2_hi, n + 1)
                        sub(D2[KR:P, :], low[0:KR, :], D2[0:KR, :].bitcast(F32)).then_inc(d2_rdy, 1)
                    if turn and nxt:
                        M = ITILES[-1]
                        dve.wait_ge(lr_hi, hi + 4)
                        sub(QDL[:, 0:NI - 1, :], qd_raw[:, 0:NI - 1, :], QDH[:, 0:NI - 1, :].bitcast(F32))
                        sub(QDL[0:M, NI - 1, :], qd_raw[0:M, NI - 1, :], QDH[0:M, NI - 1, :].bitcast(F32)).then_inc(w_qd, 1)
                    if more:
                        next_x((2, 3))
                    for i in range(4):
                        dve.wait_ge(y_done, 4 * s + i + 1)
                        acc = xtok[:, 4 * tb + i, :]
                        if i == 0 and routed:
                            dve.wait_ge(sf_rdy, f + 1)
                        after(dve, y_added, 4 * s + i + 1 - 4 * NB)
                        if routed:
                            nc.vector.scalar_tensor_tensor(acc, y_ps[i % 2][:], sf[:, 4 * tb + i:4 * tb + i + 1], acc,
                                                           ALU.mult, ALU.add).then_inc(y_added, 1)
                        else:
                            nc.vector.tensor_tensor(acc, y_ps[i % 2][:], acc, ALU.add).then_inc(y_added, 1)
                    if turn:
                        dw_split(e + 1)
                        if nxt:
                            dve.wait_ge(lr_hi, hi + 5)
                            sub(DBL[:], db_raw[0:KR, :], DBH[0:KR, :].bitcast(F32)).then_inc(w_db, 1)
            over_experts(dve, body)

        @block.tensor
        def _(pe):
            mm = nc.tensor.matmul

            def three(out, wh, wl, xh, xl, first, last):
                mm(out, wh, xh, start=first, stop=False)
                mm(out, wh, xl, start=False, stop=False)
                return mm(out, wl, xh, start=False, stop=last)

            def XE(f, tb, at, k):
                if k == 0:
                    pe.wait_ge(w_mu, f + 1)
                    pe.wait_ge(l_ws[tb % 2], 48 * (2 * f + tb // 2 + 1))
                mm(pair[slot(at, 1 + k // 2)][k % 2][:], MUS[:, k * P:(k + 1) * P], ws[:, tb % 2, :],
                   start=True, stop=True).then_inc(xe_done, 1)

            def body(e, routed, nxt):
                f = e - 2
                for tb in range(NB):
                    s, n = e * NB + tb, f * NB + tb
                    more = tb < NB - 1 or nxt is not None
                    mixed_next = (routed and tb < NB - 1) or (nxt and tb == NB - 1)
                    pe.wait_ge(xl_rdy, KC * (s + 1))
                    if routed:
                        pe.wait_ge(w_qa, f + 1)
                        after(pe, low_rdy, n)
                        for k in range(KC):
                            last = three(qa_ps[:], QAH[:, k, :], QAL[:, k, :], XH[:, k, :], XL[:, k, :], k == 0, k == KC - 1)
                        last.then_inc(qa_done, 1)
                    for j, M in enumerate(ITILES):
                        b = slot(tb, j)
                        after(pe, h_rdy, NI * s + j - 1)
                        pe.wait_ge(w_gu, NI * e + j + 1)
                        for c in range(2):
                            for k in range(KC):
                                last = three(pair[b][c][0:M, :], GUH[j][:, k, c, :], GUL[j][:, k, c, :],
                                             XH[:, k, :], XL[:, k, :], k == 0, k == KC - 1 and not routed)
                        if routed:
                            if j == 0:
                                pe.wait_ge(w_qb, f + 1)
                                pe.wait_ge(gu2_rdy, 2 * n + 2)
                            cols = slice(j * P, j * P + M)
                            for c, S2, hi in ((0, G2, slice(0, KR)), (1, U2, slice(KR, P))):
                                mm(pair[b][c][0:M, :], QBH[:, c, cols], S2[:], start=False, stop=False)
                                last = mm(pair[b][c][0:M, :], QBL[hi, cols], S2[hi, :], start=False, stop=True)
                        last.then_inc(gu_done, 1)

                    def down(i, js, first=False, stop=False):
                        out = y_ps[i % 2][:]
                        t = slice(i * P, (i + 1) * P)
                        if first:
                            after(pe, y_added, 4 * s + i - 1)
                        for j in js:
                            M = ITILES[j]
                            pe.wait_ge(hl_rdy, NI * s + j + 1)
                            last = three(out, HH[0:M, j, t], HL[0:M, j, t], DWH[0:M, j, :], DWL[0:M, j, :],
                                         first and j == js[0], stop and j == js[-1])
                        return last

                    def down_low(i):
                        out = y_ps[i % 2][:]
                        t = slice(i * P, (i + 1) * P)
                        mm(out, D2[:, t], DBH[:], start=False, stop=False)
                        mm(out, D2[0:KR, t], DBL[:], start=False, stop=True).then_inc(y_done, 1)

                    def finish(i, js, first=False):
                        last = down(i, js, first, not routed)
                        if routed:
                            down_low(i)
                        else:
                            last.then_inc(y_done, 1)

                    pe.wait_ge(w_dw, e + 1)
                    down(0, (0, 1), True)
                    if mixed_next:
                        pe.wait_ge(h_rdy, NI * s + 2)
                        XE(f + (tb + 1) // NB, (tb + 1) % NB, tb, 0)
                        XE(f + (tb + 1) // NB, (tb + 1) % NB, tb, 1)
                    if routed:
                        pe.wait_ge(w_qd, f + 1)
                        after(pe, lowd_rdy, n)
                        for j, M in enumerate(ITILES):
                            pe.wait_ge(hl_rdy, NI * s + j + 1)
                            last = three(qd_ps[0:KR, :], QDH[0:M, j, :], QDL[0:M, j, :], HH[0:M, j, :], HL[0:M, j, :],
                                         j == 0, j == NI - 1)
                        last.then_inc(qd_done, 1)
                    if mixed_next:
                        pe.wait_ge(h_rdy, NI * s + 3)
                        XE(f + (tb + 1) // NB, (tb + 1) % NB, tb, 2)
                        XE(f + (tb + 1) // NB, (tb + 1) % NB, tb, 3)
                    if routed:
                        down(0, (2,))
                        down(1, (0, 1, 2), True)
                        pe.wait_ge(w_db, f + 1)
                        pe.wait_ge(d2_rdy, n + 1)
                        down_low(0)
                        down_low(1)
                    else:
                        finish(0, (2,))
                        finish(1, (0, 1, 2), True)
                    finish(2, (0, 1, 2), True)
                    finish(3, (0, 1, 2), True)
            over_experts(pe, body)


def program(nc, A):
    with ExitStack() as ctx:
        x2T = ctx.enter_context(nc.sbuf_tensor("x2T", [P, KC, T], F32))
        xtok = ctx.enter_context(nc.sbuf_tensor("xtok", [P, NT, D], F32))
        scal = ctx.enter_context(nc.sbuf_tensor("scal", [P, NT, F], F32))
        soft_f = nc.dram_tensor("soft_f", [F, K8, T], F32).ap()
        soft_hl = nc.dram_tensor("soft_hl", [2, F, K8, T], F32).ap()
        splitter = Splitter(nc, ctx)
        with ExitStack() as mixing:
            ident = mixing.enter_context(nc.sbuf_tensor("ident", [P, P], F32))
            with nc.semaphore("ident_rdy") as ident_rdy, nc.Block() as block:
                @block.gpsimd
                def _(pool):
                    nc.gpsimd.memset(ident[:], 0.0).then_inc(ident_rdy, 1)
                    pool.wait_ge(ident_rdy, 1)
                    nc.gpsimd.affine_select(out=ident[:], in_=ident[:], compare_op=ALU.not_equal, fill=1.0,
                                            base=0, pattern=[[-1, P]], channel_multiplier=1)
            attention(nc, splitter, A, ident, x2T, xtok)
            cross(nc, splitter, A, ident, x2T, xtok)
            gating(nc, splitter, A, ident, x2T, scal, soft_f, soft_hl)
        experts(nc, A, x2T, xtok, scal, soft_f, soft_hl)
        last_norm(nc, A, xtok)


def last_norm(nc, A, xtok):
    with ExitStack() as ctx:
        def sb(name, shape):
            return ctx.enter_context(nc.sbuf_tensor(name, shape, F32))

        def sem(name):
            return ctx.enter_context(nc.semaphore(name))

        st, mv, ve, rstd, half = sb("f_st", [P, NT, 6]), sb("f_mv", [P, NT, 2]), sb("f_ve", [P, NT]), sb("f_rstd", [P, NT]), sb("f_half", [P, NT])
        stats, aggr, ve_rdy, rstd_rdy, out_rdy, stored, half_set = (sem("f_" + n) for n in ("stats", "aggr", "ve_rdy", "rstd_rdy", "out_rdy", "stored", "half_set"))
        block = ctx.enter_context(nc.Block())

        @block.vector
        def _(dve):
            for i in range(NT):
                last = nc.vector.bn_stats(st[:, i, :], xtok[:, i, :])
            last.then_inc(stats, 1)
            dve.wait_ge(stats, 1)
            for i in range(NT):
                last = nc.vector.bn_aggr(mv[:, i, :], st[:, i, :])
            last.then_inc(aggr, 1)
            dve.wait_ge(aggr, 1)
            nc.vector.tensor_scalar(ve[:].unsqueeze(2), mv[:, :, 1:2], EPS, None, ALU.add).then_inc(ve_rdy, 1)
            dve.wait_ge(rstd_rdy, 1)
            for i in range(NT):
                nc.vector.tensor_scalar(xtok[:, i, :], xtok[:, i, :], mv[:, i, 0:1], rstd[:, i:i + 1],
                                        ALU.subtract, ALU.mult).then_inc(out_rdy, 1)

        @block.gpsimd
        def _(pool):
            nc.gpsimd.memset(half[:], -0.5).then_inc(half_set, 1)
            pool.wait_ge(half_set, 1)
            pool.wait_ge(ve_rdy, 1)
            nc.gpsimd.tensor_tensor(rstd[:], ve[:], half[:], ALU.pow).then_inc(rstd_rdy, 1)

        @block.sync
        def _(sp):
            for i in range(NT):
                sp.wait_ge(out_rdy, i + 1)
                sp.dma_start(A["out"][i * P:(i + 1) * P, :], xtok[:, i, :]).then_inc(stored, 16)
            sp.wait_ge(stored, 16 * NT)


def lay_out(inputs):
    import numpy as np

    a = {n: np.asarray(v) for n, v in inputs.items()}
    ffn = lambda n: a["L0_ffn_" + n]
    by_chunk = lambda w: w.reshape(KC, P, -1).transpose(1, 0, 2)
    tokens = a["x"].reshape(T, D)
    out = {
        "x": tokens,
        "xT": tokens.reshape(T, KC, P).transpose(2, 1, 0),
        "cT": a["ctx_2048"].reshape(T, KC, P).transpose(2, 1, 0),
        "wq": by_chunk(a["L0_attn_Wq"].reshape(D, KV, G, HD).transpose(0, 2, 1, 3).reshape(D, D)),
        "wk": by_chunk(a["L0_attn_Wk"]),
        "wv": by_chunk(a["L0_attn_Wv"]),
        "wo": by_chunk(a["L0_attn_Wo"].reshape(KV, G, HD, D).transpose(1, 0, 2, 3).reshape(D, D)),
        "xb": np.stack([a["L0_xattn_b" + n].reshape(KC, P) for n in "qkv"]).transpose(2, 0, 1),
        "xbo": a["L0_xattn_bo"],
        "gate": by_chunk(ffn("gate_weight").T),
        "inv": ffn("inv_mapping").reshape(E),
    }
    for n in "qkvo":
        out["xw" + n] = by_chunk(a["L0_xattn_W" + n].T)
    pair = np.stack([np.concatenate([ffn("sh_gate_W").reshape(2, I, D), ffn("gate_W")]),
                     np.concatenate([ffn("sh_up_W").reshape(2, I, D), ffn("up_W")])])
    pair = pair.reshape(2, 2 + F, I, KC, P).transpose(1, 4, 3, 0, 2)
    out["gu"] = np.concatenate([pair[..., j * P:j * P + m].reshape(2 + F, P, -1) for j, m in enumerate(ITILES)], axis=2)
    out["dw"] = np.concatenate([ffn("sh_down_W").T.reshape(2, I, D), ffn("down_W").transpose(0, 2, 1)])
    out["mu"] = ffn("mask_up_W").transpose(0, 2, 1)
    out["qa"] = np.stack([ffn("gate_qa"), ffn("up_qa")], axis=1).reshape(F, P, KC, P).transpose(0, 3, 2, 1).reshape(F, P, D)
    out["qb"] = np.stack([ffn("gate_qb"), ffn("up_qb")], axis=1).transpose(0, 2, 4, 1, 3).reshape(F, KR, 2, I)
    out["gu_scale"] = np.stack([ffn("gate_scale"), ffn("up_scale")], axis=1).reshape(F, 2 * I)
    out["qd"] = ffn("down_qa").reshape(F, KR, I).transpose(0, 2, 1)
    out["db"] = ffn("down_qb").transpose(0, 1, 3, 2).reshape(F, KR, D)
    out["d_scale"] = ffn("down_scale")
    return {n: np.ascontiguousarray(v) for n, v in out.items()}


def kernel(**inputs):
    import concourse.bacc as bacc
    from concourse.bass_utils import run_bass_kernel_spmd

    nc = bacc.Bacc("TRN2", target_bir_lowering=False, num_devices=1)
    arrays = lay_out(inputs)
    A = {n: nc.dram_tensor("in_" + n, v.shape, mybir.dt.from_np(v.dtype), kind="ExternalInput").ap() for n, v in arrays.items()}
    A["out"] = nc.dram_tensor("out", (T, D), F32, kind="ExternalOutput").ap()
    program(nc, A)
    r = run_bass_kernel_spmd(nc, [{"in_" + n: v for n, v in arrays.items()}], core_ids=[0])
    return r.results[0]["out"].reshape(B, S, D)
```

```python
from contextlib import ExitStack

import concourse.bass as bass
from concourse import mybir

ALU = mybir.AluOpType
ACT = mybir.ActivationFunctionType
F32, F32R = mybir.dt.float32, mybir.dt.float32r
AX_X = mybir.AxisListType.X

P = 128
B, S, D = 8, 256, 512
T = B * S
NT = T // P
KC = D // P
TB = 512
NB = T // TB
F, K8, R8, I = 8, 8, 8, 352
NF = F
KR = K8 * R8
E = F * K8
TOPK = 6
ITILES = [128, 128, 96]
NI = len(ITILES)
EPS = 1e-5

KV, G, HD = 4, 4, 32
NEG = -1e30
NH = KV * G
ROWS = 104
NG = S // 8
NQ = NG // 4


def after(eng, s, count):
    if not (isinstance(count, int) and count <= 0):
        eng.wait_ge(s, count)


def over_batches(eng, body):
    body(0, True, False)
    with eng.Fori(1, B - 1) as b:
        body(b, False, False)
    body(B - 1, False, True)


class Steps:

    def __init__(self, eng, sem, per, turn):
        self.eng, self.sem, self.per, self.turn, self.n = eng, sem, per, turn, 0

    def did(self, instruction):
        instruction.then_inc(self.sem, 1)
        self.n += 1

    def settle(self):
        self.eng.wait_ge(self.sem, self.turn * self.per + self.n)

    def close(self):
        assert self.n == self.per, self.n


def alone(eng, past):
    eng.sem_inc(past, 1)


class Splitter:

    def __init__(self, nc, ctx):
        self.nc = nc
        self.landed = [ctx.enter_context(nc.semaphore(f"weights_landed{n}")) for n in range(4)]
        self.loads = [0] * 4
        self.high, self.low = ctx.enter_context(nc.semaphore("split_high")), ctx.enter_context(nc.semaphore("split_low"))
        self.done = 0

    def split(self, loads, sync=None, gpsimd=None):
        nc, before = self.nc, self.done
        with ExitStack() as ctx:
            raws = [ctx.enter_context(nc.sbuf_tensor(f"land_{hi.tensor.name}", list(hi.shape), F32)) for _, hi, _ in loads]
            block = ctx.enter_context(nc.Block())
            for n in range(len(loads)):
                self.loads[n] += 1

            @block.sync
            def _(sp):
                for n, (src, _, _) in enumerate(loads):
                    sp.dma_start(raws[n][:], src).then_inc(self.landed[n], 16)
                if sync:
                    sync(sp)

            if gpsimd:
                block.gpsimd(gpsimd)

            @block.scalar
            def _(act):
                for n, (_, hi, _) in enumerate(loads):
                    act.wait_ge(self.landed[n], 16 * self.loads[n])
                    nc.scalar.activation(hi, raws[n][:], ACT.Copy).then_inc(self.high, 1)

            @block.vector
            def _(dve):
                for n, (_, hi, lo) in enumerate(loads):
                    dve.wait_ge(self.high, before + n + 1)
                    nc.vector.tensor_tensor(lo, raws[n][:], hi.bitcast(F32), ALU.subtract).then_inc(self.low, 1)
                dve.wait_ge(self.low, before + len(loads))
            self.done += len(loads)


def attention(nc, splitter, A, ident, bo, x2T, xtok):
    with ExitStack() as ctx:
        def sb(name, shape, dt=F32):
            return ctx.enter_context(nc.sbuf_tensor(name, shape, dt))

        def sem(name):
            return ctx.enter_context(nc.semaphore(name))

        WQH, WQL = sb("WQH", [P, KC, D], F32R), sb("WQL", [P, KC, D], F32R)
        WKH, WKL = sb("WKH", [P, KC, P], F32R), sb("WKL", [P, KC, P], F32R)
        WOH, WOL = sb("WOH", [P, G, D], F32R), sb("WOL", [P, G, D], F32R)
        wv = sb("wv_sb", [P, KC, P])
        identR = sb("identR", [P, P], F32R)
        mask_f = sb("mask_f", [P, KV, P + S])
        mask0, mask1 = sb("mask0", [P, KV, P], F32R), sb("mask1", [P, 2, S], F32R)
        xT, x_in = sb("xT_raw", [P, KC, S]), sb("x_raw", [P, 2, D])
        XH, XL = sb("aXH", [P, KC, S], F32R), sb("aXL", [P, KC, S], F32R)
        QH, QL = sb("QH", [P, G, S], F32R), sb("QL", [P, G, S], F32R)
        KH, KL = sb("KH", [P, KV, S], F32R), sb("KL", [P, KV, S], F32R)
        V = sb("V", [P, 2, P])
        p0, p1 = sb("p0", [P, 2, KV, P]), sb("p1", [P, 2, KV, S])
        PT = sb("PT", [P, 2, KV, 3 * P])
        OH, OL = sb("OH", [P, G, S], F32R), sb("OL", [P, G, S], F32R)
        nm, sums, rinv = (sb(n, [P, 2, 8]) for n in ("nm", "sums", "rinv"))
        xs = sb("xs", [P, 2, D])
        st, mv, ve, rstd, half = sb("st", [P, 2, 6]), sb("mv", [P, 2, 2]), sb("ve", [P, 2]), sb("rstd", [P, 2]), sb("half", [P, 2])
        s_ps = [ctx.enter_context(nc.psum_tensor(f"s_ps{i}", [P, 512], F32)) for i in range(3)]
        t_ps = [ctx.enter_context(nc.psum_tensor(f"t_ps{i}", [P, 4, P], F32)) for i in range(3)]
        j_ps = [ctx.enter_context(nc.psum_tensor(f"j_ps{i}", [P, 512], F32)) for i in range(2)]

        l_w, l_x, l_xt = sem("l_w"), sem("l_x"), sem("l_xt")
        consts, const_r, past = sem("consts"), sem("const_r"), sem("past")
        xh_rdy, xl_rdy = sem("a_xh"), sem("a_xl")
        proj_done, hi_rdy, lo_rdy, v_rdy = sem("proj_done"), sem("hi_rdy"), sem("lo_rdy"), sem("v_rdy")
        s_done, max_rdy, exp_done, rinv_rdy, norm_rdy = (sem(n) for n in ("s_done", "max_rdy", "exp_done", "rinv_rdy", "norm_rdy"))
        t_done, pt_act, pt_dve, o_done, oh_rdy, ol_rdy = (sem(n) for n in ("t_done", "pt_act", "pt_dve", "o_done", "oh_rdy", "ol_rdy"))
        wo_done, r_rdy, ve_rdy, rstd_rdy, xs_rdy, xt_done, xt_act, xt_dve, xtok_rdy = (
            sem(n) for n in ("wo_done", "r_rdy", "ve_rdy", "rstd_rdy", "xs_rdy", "xt_done", "xt_act", "xt_dve", "xtok_rdy"))
        dve_steps = sem("dve_steps")
        NPJ = G + 2
        U = 3
        SCALE = HD ** -0.5

        def first_loads(sp):
            sp.dma_start(xT[:], A["xT"][:, :, 0:S]).then_inc(l_xt, 16)
            sp.dma_start(x_in[:], A["x"][0:S, :].rearrange("(i p) n -> p i n", p=P)).then_inc(l_x, 16)
            sp.dma_start(wv[:], A["wv"]).then_inc(l_w, 16)
            sp.dma_start(bo[:], A["xbo"].partition_broadcast(P)).then_inc(l_w, 16)

        def constants(pool):
            nc.gpsimd.memset(mask_f[:], 0.0).then_inc(consts, 1)
            nc.gpsimd.memset(half[:], -0.5).then_inc(consts, 1)
            nc.gpsimd.memset(KH[:].bitcast(F32), 0.0).then_inc(consts, 1)
            nc.gpsimd.memset(KL[:].bitcast(F32), 0.0).then_inc(consts, 1)
            pool.wait_ge(consts, 1)
            nc.gpsimd.affine_select(out=mask_f[:, :, 0:P], in_=mask_f[:, :, 0:P], compare_op=ALU.is_ge, fill=NEG,
                                    base=0, pattern=[[0, KV], [-1, P]], channel_multiplier=1).then_inc(consts, 1)
            nc.gpsimd.affine_select(out=mask_f[:, 0:2, P:P + S], in_=mask_f[:, 0:2, P:P + S], compare_op=ALU.is_ge, fill=NEG,
                                    base=P, pattern=[[0, 2], [-1, S]], channel_multiplier=1).then_inc(consts, 1)

        splitter.split([(A["wk"], WKH[:], WKL[:]), (A["wq"], WQH[:], WQL[:]), (A["wo"], WOH[:], WOL[:])], first_loads, constants)
        block = ctx.enter_context(nc.Block())

        @block.sync
        def _(sp):
            def batch(b, first, last):
                if not last:
                    sp.wait_ge(proj_done, NPJ * (b + 1))
                    alone(sp, past)
                    sp.dma_start(xT[:], A["xT"][:, :, bass.ds((b + 1) * S, S)]).then_inc(l_xt, 16)
                    sp.wait_ge(r_rdy, 2 * (b + 1))
                    alone(sp, past)
                    sp.dma_start(x_in[:], A["x"][bass.ds((b + 1) * S, S), :].rearrange("(i p) n -> p i n", p=P)).then_inc(l_x, 16)
            over_batches(sp, batch)

        @block.gpsimd
        def _(pool):
            pool.wait_ge(l_w, 32)

            def rows_out(b):
                for i in range(2):
                    pool.wait_ge(xs_rdy, 2 * b + i + 1)
                    alone(pool, past)
                    nc.gpsimd.tensor_tensor(xtok[:, bass.ds(2 * b + i, 1), :], xs[:, i:i + 1, :], bo[:].unsqueeze(1),
                                            ALU.add).then_inc(xtok_rdy, 1)

            def batch(b, first, last):
                for g in range(G):
                    u = g % 2
                    pool.wait_ge(rinv_rdy, G * b + g + 1)
                    nc.gpsimd.tensor_tensor(p0[:, u], p0[:, u], rinv[:, u, 0:4].unsqueeze(2).to_broadcast([P, KV, P]), ALU.mult)
                    nc.gpsimd.tensor_tensor(p1[:, u], p1[:, u], rinv[:, u, 4:8].unsqueeze(2).to_broadcast([P, KV, S]),
                                            ALU.mult).then_inc(norm_rdy, 1)
                    if g == 1 and not first:
                        rows_out(b - 1)
                for i in range(2):
                    pool.wait_ge(ve_rdy, 2 * b + i + 1)
                    nc.gpsimd.tensor_tensor(rstd[:, i:i + 1], ve[:, i:i + 1], half[:, i:i + 1], ALU.pow).then_inc(rstd_rdy, 1)
                if last:
                    rows_out(b)
            over_batches(pool, batch)

        @block.scalar
        def _(act):
            copy = lambda out, src: nc.scalar.activation(out, src, ACT.Copy)

            def split_x(b):
                act.wait_ge(l_xt, 16 * (b + 1))
                after(act, proj_done, NPJ * b)
                copy(XH[:], xT[:]).then_inc(xh_rdy, 1)

            def k_high(b):
                act.wait_ge(proj_done, NPJ * b + 1)
                after(act, s_done, U * G * b)
                for kv in range(KV):
                    rows = slice(HD * kv, HD * kv + HD)
                    done = copy(KH[rows, kv, :], s_ps[0][rows, 0:S])
                done.then_inc(hi_rdy, 1)

            def q_high(b, g):
                act.wait_ge(proj_done, NPJ * b + g + 2)
                nc.scalar.activation(QH[:, g, :], s_ps[(g + 1) % 3][:, 0:S], ACT.Copy, scale=SCALE).then_inc(hi_rdy, 1)

            def v_copy(b):
                act.wait_ge(proj_done, NPJ * b + NPJ)
                copy(V[:].rearrange("p i v -> p (i v)"), j_ps[0][:, 0:S]).then_inc(v_rdy, 1)

            def exps(b, g):
                u = g % 2
                for unit, kvs in enumerate(((0, 1, 2, 3), (0, 1), (2, 3))):
                    act.wait_ge(max_rdy, U * (G * b + g) + unit + 1)
                    for kv in kvs:
                        n = kv if unit == 0 else 4 + kv
                        probs, keys = (p0, P) if unit == 0 else (p1, S)
                        at = (kv - kvs[0]) * keys
                        done = nc.scalar.activation(probs[:, u, kv, :], s_ps[unit][:, at:at + keys], ACT.Exp,
                                                    bias=nm[:, u, n:n + 1], accum_out=sums[:, u, n:n + 1])
                    done.then_inc(exp_done, 1)

            def pt_copy(b, g):
                act.wait_ge(t_done, G * b + g + 1)
                copy(PT[:, g % 2, :, 0:P], t_ps[0][:])
                copy(PT[:, g % 2, :, 2 * P:3 * P], t_ps[2][:]).then_inc(pt_act, 1)

            def o_copy(b, g):
                act.wait_ge(o_done, G * b + g + 1)
                copy(OH[:, g, :], j_ps[g % 2][:, 0:S]).then_inc(oh_rdy, 1)

            def features_out(b):
                for i in range(2):
                    act.wait_ge(xt_done, 2 * b + i + 1)
                    alone(act, past)
                    copy(x2T[:, 0:2, bass.ds(b * S + i * P, P)], t_ps[i][:, 0:2, :]).then_inc(xt_act, 1)

            act.wait_ge(consts, 6)
            copy(mask0[:], mask_f[:, :, 0:P]).then_inc(const_r, 1)
            copy(mask1[:], mask_f[:, 0:2, P:P + S]).then_inc(const_r, 1)
            copy(identR[:], ident[:]).then_inc(const_r, 1)
            split_x(0)
            k_high(0)
            for g in range(G):
                q_high(0, g)

            def batch(b, first, last):
                exps(b, 0)
                if not first:
                    features_out(b - 1)
                exps(b, 1)
                v_copy(b)
                pt_copy(b, 0)
                if not last:
                    split_x(b + 1)
                exps(b, 2)
                o_copy(b, 0)
                pt_copy(b, 1)
                exps(b, 3)
                o_copy(b, 1)
                pt_copy(b, 2)
                if last:
                    o_copy(b, 2)
                    pt_copy(b, 3)
                    o_copy(b, 3)
                    features_out(b)
                else:
                    k_high(b + 1)
                    o_copy(b, 2)
                    q_high(b + 1, 0)
                    q_high(b + 1, 1)
                    pt_copy(b, 3)
                    q_high(b + 1, 2)
                    q_high(b + 1, 3)
                    o_copy(b, 3)
            over_batches(act, batch)

        @block.vector
        def _(dve):
            sub = lambda out, a, b: nc.vector.tensor_tensor(out, a, b, ALU.subtract)

            def split_x(b):
                dve.wait_ge(xh_rdy, b + 1)
                sub(XL[:], xT[:], XH[:].bitcast(F32)).then_inc(xl_rdy, 1)

            def k_low(b):
                dve.wait_ge(hi_rdy, (G + 1) * b + 1)
                for kv in range(KV):
                    rows = slice(HD * kv, HD * kv + HD)
                    done = sub(KL[rows, kv, :], s_ps[0][rows, 0:S], KH[rows, kv, :].bitcast(F32))
                done.then_inc(lo_rdy, 1)

            def q_low(b, g):
                dve.wait_ge(hi_rdy, (G + 1) * b + g + 2)
                nc.vector.scalar_tensor_tensor(QL[:, g, :], s_ps[(g + 1) % 3][:, 0:S], SCALE, QH[:, g, :].bitcast(F32),
                                               ALU.mult, ALU.subtract).then_inc(lo_rdy, 1)

            def maximum(b, g, unit):
                u = g % 2
                at, heads = ((0, 4), (4, 2), (6, 2))[unit]
                dve.wait_ge(s_done, U * (G * b + g) + unit + 1)
                nc.vector.tensor_reduce(nm[:, u, at:at + heads], s_ps[unit][:].rearrange("p (v s) -> p v s", v=heads), AX_X,
                                        ALU.max, negate=True).then_inc(max_rdy, 1)

            def reciprocals(b, g):
                u = g % 2
                dve.wait_ge(exp_done, U * (G * b + g + 1))
                nc.vector.reciprocal(rinv[:, u, :], sums[:, u, :]).then_inc(rinv_rdy, 1)

            def pt_copy(b, g):
                dve.wait_ge(t_done, G * b + g + 1)
                nc.vector.tensor_copy(PT[:, g % 2, :, P:2 * P], t_ps[1][:]).then_inc(pt_dve, 1)

            def o_low(b, g):
                dve.wait_ge(oh_rdy, G * b + g + 1)
                sub(OL[:, g, :], j_ps[g % 2][:, 0:S], OH[:, g, :].bitcast(F32)).then_inc(ol_rdy, 1)

            def norm_out(b):
                for i in range(2):
                    dve.wait_ge(rstd_rdy, 2 * b + i + 1)
                    nc.vector.tensor_scalar(xs[:, i, :], xs[:, i, :], mv[:, i, 0:1], rstd[:, i:i + 1],
                                            ALU.subtract, ALU.mult).then_inc(xs_rdy, 1)

            def features_out(b):
                for i in range(2):
                    dve.wait_ge(xt_act, 2 * b + i + 1)
                    alone(dve, past)
                    nc.vector.tensor_copy(x2T[:, 2:4, bass.ds(b * S + i * P, P)], t_ps[i][:, 2:4, :]).then_inc(xt_dve, 1)

            split_x(0)
            k_low(0)
            for g in range(G):
                q_low(0, g)

            def batch(b, first, last):
                own = Steps(dve, dve_steps, 2 * 2, b)
                def maxima(g):
                    for unit in range(U):
                        maximum(b, g, unit)

                maximum(b, 0, 0)
                if not first:
                    norm_out(b - 1)
                maximum(b, 0, 1)
                maximum(b, 0, 2)
                if not first:
                    features_out(b - 1)
                reciprocals(b, 0)
                maxima(1)
                reciprocals(b, 1)
                pt_copy(b, 0)
                maxima(2)
                if not last:
                    split_x(b + 1)
                reciprocals(b, 2)
                o_low(b, 0)
                pt_copy(b, 1)
                maxima(3)
                reciprocals(b, 3)
                o_low(b, 1)
                pt_copy(b, 2)
                if not last:
                    k_low(b + 1)
                o_low(b, 2)
                if not last:
                    q_low(b + 1, 0)
                    q_low(b + 1, 1)
                pt_copy(b, 3)
                if not last:
                    q_low(b + 1, 2)
                    q_low(b + 1, 3)
                o_low(b, 3)
                dve.wait_ge(l_x, 16 * (b + 1))
                after(dve, xtok_rdy, 2 * b)
                for i in range(2):
                    dve.wait_ge(wo_done, 2 * b + i + 1)
                    nc.vector.tensor_tensor(xs[:, i, :], j_ps[i][:], x_in[:, i, :], ALU.add).then_inc(r_rdy, 1)
                    dve.wait_ge(r_rdy, 2 * b + i + 1)
                    own.did(nc.vector.bn_stats(st[:, i, :], xs[:, i, :]))
                    own.settle()
                    alone(dve, past)
                    own.did(nc.vector.bn_aggr(mv[:, i, :], st[:, i, :]))
                    own.settle()
                    nc.vector.tensor_scalar(ve[:, i:i + 1], mv[:, i, 1:2], EPS, None, ALU.add).then_inc(ve_rdy, 1)
                own.close()
                if last:
                    norm_out(b)
                    features_out(b)
            over_batches(dve, batch)

        @block.tensor
        def _(pe):
            mm = nc.tensor.matmul

            def three(out, wh, wl, xh, xl, first, last):
                mm(out, wh, xh, start=first, stop=False)
                mm(out, wh, xl, start=False, stop=False)
                return mm(out, wl, xh, start=False, stop=last)

            def keys(b):
                pe.wait_ge(xl_rdy, b + 1)
                after(pe, exp_done, U * (G * b - 1) + 1 if not isinstance(b, int) or b else 0)
                for k in range(KC):
                    done = three(s_ps[0][:, 0:S], WKH[:, k, :], WKL[:, k, :], XH[:, k, :], XL[:, k, :], k == 0, k == KC - 1)
                done.then_inc(proj_done, 1)

            def queries(b, g):
                if g < 2:
                    after(pe, exp_done, U * (G * b - 1) + g + 2 if not isinstance(b, int) or b else 0)
                else:
                    pe.wait_ge(lo_rdy, (G + 1) * b + g - 1)
                for k in range(KC):
                    c = slice(g * P, (g + 1) * P)
                    done = three(s_ps[(g + 1) % 3][:, 0:S], WQH[:, k, c], WQL[:, k, c], XH[:, k, :], XL[:, k, :], k == 0, k == KC - 1)
                done.then_inc(proj_done, 1)

            def vals(b):
                after(pe, r_rdy, 2 * b - 1)
                for i in range(2):
                    for k in range(KC):
                        done = mm(j_ps[0][:, i * P:(i + 1) * P], xT[:, k, i * P:(i + 1) * P], wv[:, k, :],
                                  start=(k == 0), stop=(k == KC - 1), skip_group_check=True)
                done.then_inc(proj_done, 1)

            def scores(b, g):
                for unit, i, kv, keys, m in ((0, 0, slice(0, 4), slice(0, P), mask0), (1, 1, slice(0, 2), slice(0, S), mask1),
                                             (2, 1, slice(2, 4), slice(0, S), mask1)):
                    if g >= 1:
                        pe.wait_ge(exp_done, U * (G * b + g - 1) + unit + 1)
                    elif unit == 0:
                        pe.wait_ge(lo_rdy, (G + 1) * (b + 1))
                    q = slice(i * P, (i + 1) * P)
                    out = s_ps[unit][:].rearrange("p (v s) -> p v s", v=4 if unit == 0 else 2)
                    three(out, QH[:, g, q], QL[:, g, q], KH[:, kv, keys], KL[:, kv, keys], True, False)
                    mm(out, identR[:], m[:], start=False, stop=True).then_inc(s_done, 1)

            def turn(b, g):
                u = g % 2
                pe.wait_ge(norm_rdy, G * b + g + 1)
                after(pe, pt_act, G * b + g)
                after(pe, pt_dve, G * b + g)
                if g == 0:
                    after(pe, xt_dve, 2 * b)
                for kv in range(KV):
                    nc.tensor.transpose(t_ps[0][:, kv, :], p0[:, u, kv, :], ident[:])
                    nc.tensor.transpose(t_ps[1][:, kv, :], p1[:, u, kv, 0:P], ident[:])
                    done = nc.tensor.transpose(t_ps[2][:, kv, :], p1[:, u, kv, P:S], ident[:])
                done.then_inc(t_done, 1)

            def values(b, g):
                u = g % 2
                pe.wait_ge(pt_act, G * b + g + 1)
                pe.wait_ge(pt_dve, G * b + g + 1)
                if g == 0:
                    pe.wait_ge(v_rdy, b + 1)
                if g < 2:
                    after(pe, r_rdy, 2 * b)
                else:
                    pe.wait_ge(ol_rdy, G * b + g - 1)
                for kv in range(KV):
                    mm(j_ps[g % 2][HD * kv:HD * kv + HD, 0:S], V[:, 0, HD * kv:HD * kv + HD], PT[:, u, kv, 0:S],
                       start=True, stop=False)
                for kv in range(KV):
                    done = mm(j_ps[g % 2][HD * kv:HD * kv + HD, P:S], V[:, 1, HD * kv:HD * kv + HD], PT[:, u, kv, S:S + P],
                              start=False, stop=True)
                done.then_inc(o_done, 1)

            def outputs(b):
                for i in range(2):
                    for g in range(G):
                        t = slice(i * P, (i + 1) * P)
                        if i == 0:
                            pe.wait_ge(ol_rdy, G * b + g + 1)
                        done = three(j_ps[i][:], OH[:, g, t], OL[:, g, t], WOH[:, g, :], WOL[:, g, :], g == 0, g == G - 1)
                    done.then_inc(wo_done, 1)

            def turn_rows(b):
                pe.wait_ge(pt_act, G * (b + 1))
                pe.wait_ge(pt_dve, G * (b + 1))
                for i in range(2):
                    pe.wait_ge(xs_rdy, 2 * b + i + 1)
                    for c in range(KC):
                        done = nc.tensor.transpose(t_ps[i][:, c, :], xs[:, i, c * P:(c + 1) * P], ident[:])
                    done.then_inc(xt_done, 1)

            pe.wait_ge(l_w, 32)
            pe.wait_ge(const_r, 3)
            keys(0)
            for g in range(G):
                queries(0, g)

            def batch(b, first, last):
                scores(b, 0)
                if not first:
                    turn_rows(b - 1)
                scores(b, 1)
                vals(b)
                turn(b, 0)
                scores(b, 2)
                values(b, 0)
                turn(b, 1)
                scores(b, 3)
                values(b, 1)
                turn(b, 2)
                if last:
                    values(b, 2)
                    turn(b, 3)
                    values(b, 3)
                else:
                    keys(b + 1)
                    values(b, 2)
                    queries(b + 1, 0)
                    queries(b + 1, 1)
                    turn(b, 3)
                    queries(b + 1, 2)
                    queries(b + 1, 3)
                    values(b, 3)
                outputs(b)
                if last:
                    turn_rows(b)
            over_batches(pe, batch)


def cross(nc, splitter, A, ident, x2T, xtok):
    with ExitStack() as ctx:
        def sb(name, shape, dt=F32):
            return ctx.enter_context(nc.sbuf_tensor(name, shape, dt))

        def sem(name):
            return ctx.enter_context(nc.semaphore(name))

        WH = [sb(f"xW{n}H", [P, KC, D], F32R) for n in "qkv"]
        WL = [sb(f"xW{n}L", [P, KC, D], F32R) for n in "qkv"]
        WOH, WOL = sb("xWoH", [P, KC, D], F32R), sb("xWoL", [P, KC, D], F32R)
        KS, QG = sb("KS", [ROWS, 2, NH, P]), sb("QG", [ROWS, 2, 4, P])
        c_raw, half, bias = sb("c_raw", [P, KC, S]), sb("xhalf", [P, 2]), sb("bias", [P, 3, KC])
        l_c, l_b, consts = sem("l_c"), sem("l_b"), sem("x_consts")

        def first_loads(sp):
            sp.dma_start(bias[:], A["xb"]).then_inc(l_b, 16)
            sp.dma_start(c_raw[:], A["cT"][:, :, 0:S]).then_inc(l_c, 16)

        def constants(pool):
            nc.gpsimd.memset(half[:], -0.5).then_inc(consts, 1)
            nc.gpsimd.memset(QG[:], 0.0).then_inc(consts, 1)
            nc.gpsimd.memset(KS[:], 0.0).then_inc(consts, 1)
            pool.wait_ge(consts, 3)
            nc.gpsimd.memset(KS[0:8, :, :, :], NEG).then_inc(consts, 1)
            pool.wait_ge(consts, 4)
            for part, fill in ((QG[0:8, :, :, :].rearrange("p s a (h t) -> p (s a h) t", t=8), 1.0),
                               (KS[0:8, :, :, :].rearrange("p s h (a t) -> p (s h a) t", t=8), 0.0)):
                nc.gpsimd.affine_select(out=part, in_=part, compare_op=ALU.not_equal, fill=fill, base=0,
                                        pattern=[[0, part.shape[1]], [1, 8]], channel_multiplier=-1).then_inc(consts, 1)
        splitter.split([(A["xw" + "qkv"[n]], WH[n][:], WL[n][:]) for n in (1, 2, 0)] + [(A["xwo"], WOH[:], WOL[:])],
                       first_loads, constants)
        XH, XL = sb("xXH", [P, KC, S], F32R), sb("xXL", [P, KC, S], F32R)
        OH, OL = sb("xOH", [P, KC, P], F32R), sb("xOL", [P, KC, P], F32R)
        FM = [sb(f"fm{n}", [P, KC, S]) for n in "qkv"]
        QS = sb("QS", [2 * HD, 2, NH, P])
        pr, PT = sb("pr", [P, 2, 4, P]), sb("xPT", [P, 2, 4, P])
        VG = sb("VG", [P, 4, 4, HD])
        nm, sums, rinv = (sb("x" + n, [P, 2, 4]) for n in ("nm", "sums", "rinv"))
        xs = sb("xxs", [P, 2, D])
        st, mv, ve, rstd = sb("xst", [P, 2, 6]), sb("xmv", [P, 2, 2]), sb("xve", [P, 2]), sb("xrstd", [P, 2])
        s_ps = [ctx.enter_context(nc.psum_tensor(f"xs_ps{i}", [P, 4, P], F32)) for i in range(2)]
        t_ps, v_ps = (ctx.enter_context(nc.psum_tensor(f"x{n}_ps", shape, F32)) for n, shape in (("t", [P, 4, P]), ("v", [P, P])))
        o_ps, j_ps = ([ctx.enter_context(nc.psum_tensor(f"x{n}_ps{i}", [P, 512], F32)) for i in range(2)] for n in "oj")

        onehot_in = sem("onehot_in")
        l_ks, l_vs, l_qs = ([sem(f"l_{n}s{i}") for i in range(2)] for n in "kvq")
        past = sem("x_past")
        xh_rdy, xl_rdy = sem("x_xh"), sem("x_xl")
        proj_done, k_rdy, v_rdy, q_rdy = sem("x_proj"), sem("k_rdy"), sem("xv_rdy"), sem("q_rdy")
        qg_rdy, vt_done, vg_rdy = sem("qg_rdy"), sem("vt_done"), sem("vg_rdy")
        s_done, max_rdy, exp_done, rinv_rdy, norm_rdy = (sem("x_" + n) for n in ("s_done", "max_rdy", "exp_done", "rinv_rdy", "norm_rdy"))
        t_done, pt_rdy, o_done, oh_rdy, ol_rdy = (sem("x_" + n) for n in ("t_done", "pt_rdy", "o_done", "oh_rdy", "ol_rdy"))
        wo_done, r_rdy, ve_rdy, rstd_rdy, xs_rdy, xt_done, xt_act, xt_dve, xtok_rdy = (
            sem("x_" + n) for n in ("wo_done", "r_rdy", "ve_rdy", "rstd_rdy", "xs_rdy", "xt_done", "xt_act", "xt_dve", "xtok_rdy"))
        dve_steps = sem("x_dve_steps")
        NPJ = 3 * KC
        HQ = NQ // 2
        PROJECTED = [[(0, 0), (0, 1)], [(0, 2), (0, 3), (1, 0)], [(1, 1), (1, 2), (1, 3)], [(2, 0), (2, 1)],
                     [(2, 2), (2, 3)], [], [], []]
        block = ctx.enter_context(nc.Block())

        @block.sync
        def _(sp):
            def context(b):
                after(sp, xl_rdy, 2 * b - 1)
                alone(sp, past)
                sp.dma_start(c_raw[:], A["cT"][:, :, bass.ds(b * S, S)]).then_inc(l_c, 16)

            def stack(b, slot):
                after(sp, vt_done, NQ * (b - 1) + HQ * (slot + 1))
                alone(sp, past)
                for rows, to, fm, ready, landed in ((0, KS, FM[1], k_rdy, l_ks), (HD, QS, FM[2], v_rdy, l_vs),
                                                    (0, QS, FM[0], q_rdy, l_qs)):
                    sp.wait_ge(ready, KC * (b + 1))
                    for j in range(4):
                        sp.dma_start(to[rows:rows + HD, slot, j:NH:4, :],
                                     fm[HD * j:HD * j + HD, :, slot * P:slot * P + P]).then_inc(landed[slot], 16)

            sp.wait_ge(consts, 6)
            sp.dma_start(QG[96:ROWS, :, :, :], QG[0:8, :, :, :]).then_inc(onehot_in, 16)
            sp.dma_start(KS[96:ROWS, :, :, :], KS[0:8, :, :, :]).then_inc(onehot_in, 16)
            sp.wait_ge(onehot_in, 32)
            stack(0, 0)

            def batch(b, first, last):
                if not last:
                    context(b + 1)
                stack(b, 1)
                if not last:
                    stack(b + 1, 0)
            over_batches(sp, batch)

        @block.gpsimd
        def _(pool):
            def divide(b, q):
                pool.wait_ge(rinv_rdy, NQ * b + q + 1)
                nc.gpsimd.tensor_tensor(pr[:, q % 2, :, :], pr[:, q % 2, :, :], rinv[:, q % 2, :].unsqueeze(2).to_broadcast([P, 4, P]),
                                        ALU.mult).then_inc(norm_rdy, 1)

            def deviation(b, i):
                pool.wait_ge(ve_rdy, 2 * b + i + 1)
                nc.gpsimd.tensor_tensor(rstd[:, i:i + 1], ve[:, i:i + 1], half[:, i:i + 1], ALU.pow).then_inc(rstd_rdy, 1)

            def rows_out(b, i):
                pool.wait_ge(xs_rdy, 2 * b + i + 1)
                alone(pool, past)
                nc.gpsimd.tensor_copy(xtok[:, bass.ds(2 * b + i, 1), :], xs[:, i:i + 1, :]).then_inc(xtok_rdy, 1)

            divide(0, 0)

            def batch(b, first, last):
                for q in range(NQ):
                    if q + 1 < NQ:
                        divide(b, q + 1)
                    if q in (0, 2) and not first:
                        deviation(b - 1, q // 2)
                    if q in (2, 4) and not first:
                        rows_out(b - 1, q // 2 - 1)
                if last:
                    deviation(b, 0)
                    rows_out(b, 0)
                    deviation(b, 1)
                    rows_out(b, 1)
                else:
                    divide(b + 1, 0)
            over_batches(pool, batch)

        @block.scalar
        def _(act):
            copy = lambda out, src: nc.scalar.activation(out, src, ACT.Copy)

            def context_high(b):
                act.wait_ge(l_c, 16 * (b + 1))
                after(act, proj_done, NPJ * b)
                copy(XH[:], c_raw[:]).then_inc(xh_rdy, 1)

            def values_out(b, c):
                act.wait_ge(proj_done, NPJ * b + KC + c + 1)
                if c == 0:
                    for slot in range(2):
                        after(act, l_vs[slot], 64 * b)
                nc.scalar.activation(FM[2][:, c, :], j_ps[c % 2][:, 0:S], ACT.Identity, bias=bias[:, 2, c:c + 1]).then_inc(v_rdy, 1)

            def x_high(b):
                act.wait_ge(proj_done, NPJ * b + 2 * KC)
                copy(XH[:], x2T[:, :, bass.ds(b * S, S)]).then_inc(xh_rdy, 1)

            def exps(b, q):
                u = q % 2
                act.wait_ge(max_rdy, NQ * b + q + 1)
                after(act, t_done, NQ * b + q - 1)
                for a in range(4):
                    done = nc.scalar.activation(pr[:, u, a, :], s_ps[u][:, a, :], ACT.Exp, bias=nm[:, u, a:a + 1], accum_out=sums[:, u, a:a + 1])
                done.then_inc(exp_done, 1)

            def group_values(b, q):
                act.wait_ge(vt_done, NQ * b + q + 1)
                after(act, o_done, NQ * b + q - 3)
                copy(VG[:, q % 4, :, :].rearrange("p a d -> p (a d)"), v_ps[:]).then_inc(vg_rdy, 1)

            def o_high(b, i):
                act.wait_ge(o_done, NQ * b + (i + 1) * HQ)
                after(act, wo_done, 2 * b + i)
                copy(OH[:], o_ps[i][:].rearrange("p (i t) -> p i t", i=KC)).then_inc(oh_rdy, 1)

            def features_out(b, i):
                act.wait_ge(xt_done, 2 * b + i + 1)
                alone(act, past)
                copy(x2T[:, 0:2, bass.ds(b * S + i * P, P)], t_ps[:, 0:2, :]).then_inc(xt_act, 1)

            act.wait_ge(l_b, 16)
            context_high(0)
            for c in range(KC):
                values_out(0, c)
            x_high(0)
            group_values(0, 0)
            exps(0, 0)
            group_values(0, 1)
            exps(0, 1)

            def batch(b, first, last):
                for q in range(NQ):
                    if q == 0 and not last:
                        context_high(b + 1)
                    if q == 5:
                        o_high(b, 0)
                    if q + 2 < NQ:
                        group_values(b, q + 2)
                        exps(b, q + 2)
                    if not last:
                        for rank, c in PROJECTED[q]:
                            if rank == 1:
                                values_out(b + 1, c)
                            if (rank, c) == (1, KC - 1):
                                x_high(b + 1)
                    if q in (2, 4) and not first:
                        features_out(b - 1, q // 2 - 1)
                if not last:
                    group_values(b + 1, 0)
                    exps(b + 1, 0)
                    o_high(b, 1)
                    group_values(b + 1, 1)
                    exps(b + 1, 1)
                if last:
                    features_out(b, 0)
                    o_high(b, 1)
                    features_out(b, 1)
            over_batches(act, batch)

        @block.vector
        def _(dve):
            sub = lambda out, a, b: nc.vector.tensor_tensor(out, a, b, ALU.subtract)

            def context_low(b):
                dve.wait_ge(xh_rdy, 2 * b + 1)
                sub(XL[:], c_raw[:], XH[:].bitcast(F32)).then_inc(xl_rdy, 1)

            def x_low(b):
                dve.wait_ge(xh_rdy, 2 * b + 2)
                sub(XL[:], x2T[:, :, bass.ds(b * S, S)], XH[:].bitcast(F32)).then_inc(xl_rdy, 1)

            def project_out(b, n, rank, ready, moved, c):
                dve.wait_ge(proj_done, NPJ * b + rank * KC + c + 1)
                if c == 0:
                    for slot in range(2):
                        after(dve, moved[slot], 64 * b)
                nc.vector.tensor_scalar(FM[n][:, c, :], j_ps[c % 2][:, 0:S], bias[:, n, c:c + 1], None, ALU.add).then_inc(ready, 1)

            keys_out = lambda b, c: project_out(b, 1, 0, k_rdy, l_ks, c)
            queries_out = lambda b, c: project_out(b, 0, 2, q_rdy, l_qs, c)

            def group_queries(b, q):
                slot, at = q // HQ, q % HQ * 32
                if q % HQ == 0:
                    dve.wait_ge(l_vs[slot], 64 * (b + 1))
                    dve.wait_ge(l_qs[slot], 64 * (b + 1))
                after(dve, vt_done, NQ * b + q - 1)
                nc.vector.tensor_copy(QG[0:2 * HD, q % 2, :, :].rearrange("p a (h t) -> p a h t", t=8),
                                      QS[:, slot, :, at:at + 32].rearrange("p h (a t) -> p a h t", t=8)).then_inc(qg_rdy, 1)

            def maxima(b, q):
                dve.wait_ge(s_done, NQ * b + q + 1)
                nc.vector.tensor_reduce(nm[:, q % 2, :], s_ps[q % 2][:], AX_X, ALU.max, negate=True).then_inc(max_rdy, 1)

            def reciprocals(b, q):
                dve.wait_ge(exp_done, NQ * b + q + 1)
                nc.vector.reciprocal(rinv[:, q % 2, :], sums[:, q % 2, :]).then_inc(rinv_rdy, 1)

            def pt_copy(b, q):
                dve.wait_ge(t_done, NQ * b + q + 1)
                nc.vector.tensor_copy(PT[:, q % 2, :, :], t_ps[:]).then_inc(pt_rdy, 1)

            def o_low(b, i):
                dve.wait_ge(oh_rdy, 2 * b + i + 1)
                sub(OL[:], o_ps[i][:].rearrange("p (i t) -> p i t", i=KC), OH[:].bitcast(F32)).then_inc(ol_rdy, 1)

            def residual(b, i, own):
                dve.wait_ge(wo_done, 2 * b + i + 1)
                after(dve, xt_done, 2 * (b - 1) + i + 1)
                after(dve, xtok_rdy, 2 * (b - 1) + i + 1)
                nc.vector.tensor_tensor(xs[:, i:i + 1, :], j_ps[i][:].unsqueeze(1), xtok[:, bass.ds(2 * b + i, 1), :],
                                        ALU.add).then_inc(r_rdy, 1)
                dve.wait_ge(r_rdy, 2 * b + i + 1)
                own.did(nc.vector.bn_stats(st[:, i, :], xs[:, i, :]))
                own.settle()
                alone(dve, past)
                own.did(nc.vector.bn_aggr(mv[:, i, :], st[:, i, :]))
                own.settle()
                nc.vector.tensor_scalar(ve[:, i:i + 1], mv[:, i, 1:2], EPS, None, ALU.add).then_inc(ve_rdy, 1)

            def norm_out(b, i):
                dve.wait_ge(rstd_rdy, 2 * b + i + 1)
                nc.vector.tensor_scalar(xs[:, i, :], xs[:, i, :], mv[:, i, 0:1], rstd[:, i:i + 1],
                                        ALU.subtract, ALU.mult).then_inc(xs_rdy, 1)

            def features_out(b, i):
                dve.wait_ge(xt_act, 2 * b + i + 1)
                alone(dve, past)
                nc.vector.tensor_copy(x2T[:, 2:4, bass.ds(b * S + i * P, P)], t_ps[:, 2:4, :]).then_inc(xt_dve, 1)

            dve.wait_ge(l_b, 16)
            context_low(0)
            for c in range(KC):
                keys_out(0, c)
            x_low(0)
            for c in range(KC):
                queries_out(0, c)
            group_queries(0, 0)
            group_queries(0, 1)
            maxima(0, 0)
            reciprocals(0, 0)
            maxima(0, 1)
            group_queries(0, 2)

            def batch(b, first, last):
                late = Steps(dve, dve_steps, 4, b - 1)
                late.n = 2
                own = Steps(dve, dve_steps, 4, b)
                for q in range(NQ):
                    if q == 0 and not last:
                        context_low(b + 1)
                    if q + 1 < NQ:
                        reciprocals(b, q + 1)
                    if q + 2 < NQ:
                        maxima(b, q + 2)
                    elif q == NQ - 1 and not last:
                        maxima(b + 1, 0)
                    if q in (1, 3) and not first:
                        norm_out(b - 1, q // 2)
                    if q == 3 and not last:
                        x_low(b + 1)
                    if q + 3 < NQ:
                        group_queries(b, q + 3)
                    pt_copy(b, q)
                    if q >= NQ - 2 and not last:
                        group_queries(b + 1, q - (NQ - 2))
                    if q == 0 and not first:
                        residual(b - 1, 1, late)
                    if not last:
                        for rank, c in PROJECTED[q]:
                            if rank != 1:
                                (keys_out, None, queries_out)[rank](b + 1, c)
                    if q in (2, 4) and not first:
                        features_out(b - 1, q // 2 - 1)
                    if q == 5:
                        o_low(b, 0)
                if last:
                    residual(b, 0, own)
                    norm_out(b, 0)
                    features_out(b, 0)
                    o_low(b, 1)
                    residual(b, 1, own)
                    norm_out(b, 1)
                    features_out(b, 1)
                else:
                    reciprocals(b + 1, 0)
                    o_low(b, 1)
                    maxima(b + 1, 1)
                    group_queries(b + 1, 2)
                    residual(b, 0, own)
            over_batches(dve, batch)

        @block.tensor
        def _(pe):
            mm = nc.tensor.matmul

            def three(out, wh, wl, xh, xl, first, last):
                mm(out, wh, xh, start=first, stop=False)
                mm(out, wh, xl, start=False, stop=False)
                return mm(out, wl, xh, start=False, stop=last)

            def project(b, rank, c):
                if rank == 0 and c < 2:
                    pe.wait_ge(xl_rdy, 2 * b + 1)
                    after(pe, r_rdy, 2 * (b - 2) + c + 1)
                elif rank == 0 or rank == 1 and c < 2:
                    pe.wait_ge(k_rdy, KC * b + rank * KC + c - 1)
                elif rank == 1 or c < 2:
                    pe.wait_ge(v_rdy, KC * b + (rank - 1) * KC + c - 1)
                else:
                    pe.wait_ge(q_rdy, KC * b + c - 1)
                if rank == 2:
                    pe.wait_ge(xl_rdy, 2 * b + 2)
                n = (1, 2, 0)[rank]
                cols = slice(c * P, (c + 1) * P)
                for k in range(KC):
                    done = three(j_ps[c % 2][:, 0:S], WH[n][:, k, cols], WL[n][:, k, cols], XH[:, k, :], XL[:, k, :],
                                 k == 0, k == KC - 1)
                done.then_inc(proj_done, 1)

            def scores(b, q):
                slot, u = q // HQ, q % 2
                if q % HQ == 0:
                    pe.wait_ge(l_ks[slot], 64 * (b + 1))
                pe.wait_ge(qg_rdy, NQ * b + q + 1)
                after(pe, exp_done, NQ * b + q - 1)
                after(pe, vg_rdy, NQ * b + q)
                for a in range(4):
                    t = (4 * (q % HQ) + a) * 8
                    done = mm(s_ps[u][:, a, :], QG[:, u, a, :], KS[:, slot, :, t:t + 8], start=True, stop=True)
                done.then_inc(s_done, 1)
                for a in range(4):
                    done = nc.tensor.transpose(v_ps[:, a * HD:(a + 1) * HD], QG[32:64, u, a, :], ident[32:64, 32:64])
                done.then_inc(vt_done, 1)

            def turn(b, q):
                pe.wait_ge(norm_rdy, NQ * b + q + 1)
                after(pe, pt_rdy, NQ * b + q)
                if q == 3:
                    after(pe, xt_dve, 2 * (b - 1) + 1)
                if q == 5:
                    after(pe, xt_dve, 2 * b)
                for a in range(4):
                    done = nc.tensor.transpose(t_ps[:, a, :], pr[:, q % 2, a, :], ident[:])
                done.then_inc(t_done, 1)

            def values(b, q):
                pe.wait_ge(pt_rdy, NQ * b + q + 1)
                pe.wait_ge(vg_rdy, NQ * b + q + 1)
                if q % HQ == 0:
                    after(pe, ol_rdy, 2 * (b - 1) + q // HQ + 1)
                out = o_ps[q // HQ][:].rearrange("p (i t) -> p i t", i=KC)
                for a in range(4):
                    t = slice((4 * (q % HQ) + a) * 8, (4 * (q % HQ) + a) * 8 + 8)
                    probs = PT[:, q % 2, a, :].rearrange("p (i j t) -> p i j t", i=4, j=4)
                    for j in range(4):
                        done = mm(out[HD * j:HD * j + HD, :, t], VG[:, q % 4, a, :], probs[:, :, j, :], start=True, stop=True)
                done.then_inc(o_done, 1)

            def outputs(b, i, projected):
                pe.wait_ge(ol_rdy, 2 * b + i + 1)
                if projected:
                    pe.wait_ge(q_rdy, KC * (b + 1) + 3 + i)
                else:
                    after(pe, r_rdy, 2 * (b - 1) + i + 1)
                for k in range(KC):
                    done = three(j_ps[i][:], OH[:, k, :], OL[:, k, :], WOH[:, k, :], WOL[:, k, :], k == 0, k == KC - 1)
                done.then_inc(wo_done, 1)

            def turn_rows(b, i, turned):
                pe.wait_ge(xs_rdy, 2 * b + i + 1)
                pe.wait_ge(pt_rdy, turned)
                if i == 1:
                    pe.wait_ge(xt_dve, 2 * b + 1)
                for c in range(KC):
                    done = nc.tensor.transpose(t_ps[:, c, :], xs[:, i, c * P:(c + 1) * P], ident[:])
                done.then_inc(xt_done, 1)

            for rank in range(3):
                for c in range(KC):
                    project(0, rank, c)
            pe.wait_ge(onehot_in, 32)
            scores(0, 0)
            scores(0, 1)

            def batch(b, first, last):
                for q in range(NQ):
                    if q + 2 < NQ:
                        scores(b, q + 2)
                    elif q == NQ - 1 and not last:
                        scores(b + 1, 0)
                    turn(b, q)
                    if q >= 1:
                        values(b, q - 1)
                    if q == 0 and not first:
                        outputs(b - 1, 1, True)
                    if q == 7:
                        outputs(b, 0, not last)
                    if not last:
                        for rank, c in PROJECTED[q]:
                            project(b + 1, rank, c)
                    if q in (2, 4) and not first:
                        turn_rows(b - 1, q // 2 - 1, NQ * b + q + 1)
                if last:
                    values(b, NQ - 1)
                    turn_rows(b, 0, NQ * (b + 1))
                    outputs(b, 1, False)
                    turn_rows(b, 1, NQ * (b + 1))
                else:
                    values(b, NQ - 1)
                    scores(b + 1, 1)
            over_batches(pe, batch)


def gating(nc, splitter, A, ident, x2T, scal, soft_f, soft_hl, prefetch):
    with ExitStack() as ctx:
        def sb(name, shape, dt=F32):
            return ctx.enter_context(nc.sbuf_tensor(name, shape, dt))

        def sem(name):
            return ctx.enter_context(nc.semaphore(name))

        GH, GL = sb("GH", [P, KC, E], F32R), sb("GL", [P, KC, E], F32R)
        splitter.split([(A["gate"], GH[:], GL[:])])
        XH, XL = sb("gXH", [P, 2, KC, TB], F32R), sb("gXL", [P, 2, KC, TB], F32R)
        lgT = sb("lgT", [E, T])
        sc, ex, wd, flat = (sb(n, [P, NT, E]) for n in ("sc", "ex", "wd", "flat"))
        ext = sb("ext", [P, NT, E + 2])
        rest = sb("rest", [P, NT, E + 2])
        top = sb("top", [P, NT, 8])
        col, col2 = sb("col", [P, NT, F]), sb("col2", [P, NT, F])
        wdT, softT, soft_h, soft_l = sb("wdT", [E, T]), sb("softT", [E, T]), sb("soft_h", [E, T], F32R), sb("soft_l", [E, T], F32R)
        inv_i, inv_f, neg, row, sel = sb("inv_i", [E, E], mybir.dt.int32), sb("inv_f", [E, E]), sb("neg", [E, E]), sb("row", [E, 1]), sb("sel", [E, E])
        row_i = sb("row_i", [E, 1], mybir.dt.int32)
        lg_ps = [ctx.enter_context(nc.psum_tensor(f"lg_ps{i}", [P, TB], F32)) for i in range(2)]
        tok_ps = [ctx.enter_context(nc.psum_tensor(f"tok_ps{i}", [P, 8, E], F32)) for i in range(2)]
        tr_ps = [ctx.enter_context(nc.psum_tensor(f"tr_ps{i}", [P, TB], F32)) for i in range(2)]

        l_inv, stored, iota_in = sem("l_inv"), sem("stored"), sem("iota_in")
        xh_rdy, xl_rdy, lg_done, lg_rdy, tok_done = (sem("g_" + n) for n in ("xh", "xl", "lg_done", "lg_rdy", "tok_done"))
        ex_rdy, soft_e, steps, wd_rdy, wdT_done, wdT_rdy, flat_done, z_rdy, z_exp, soft_rdy, sT_done, sT_rdy, h_rdy, l_rdy = (
            sem("g_" + n) for n in ("ex_rdy", "soft_e", "steps", "wd_rdy", "wdT_done", "wdT_rdy", "flat_done", "z_rdy", "z_exp",
                                    "soft_rdy", "sT_done", "sT_rdy", "h_rdy", "l_rdy"))
        block = ctx.enter_context(nc.Block())

        @block.sync
        def _(sp):
            sp.dma_start(inv_i[:], A["inv"].partition_broadcast(E)).then_inc(l_inv, 16)
            prefetch(sp)
            sp.wait_ge(sT_rdy, NB)
            sp.dma_start(soft_f.rearrange("f k t -> (f k) t"), softT[:]).then_inc(stored, 16)
            sp.wait_ge(h_rdy, 1)
            sp.dma_start(soft_hl[0].rearrange("f k t -> (f k) t"), soft_h[:].bitcast(F32)).then_inc(stored, 16)
            sp.wait_ge(l_rdy, 1)
            sp.dma_start(soft_hl[1].rearrange("f k t -> (f k) t"), soft_l[:].bitcast(F32)).then_inc(stored, 16)
            sp.wait_ge(stored, 48)

        @block.gpsimd
        def _(pool):
            nc.gpsimd.iota(row_i[:], pattern=[[0, 1]], base=0, channel_multiplier=1).then_inc(iota_in, 1)

        @block.scalar
        def _(act):
            copy = lambda out, src: nc.scalar.activation(out, src, ACT.Copy)
            for tb in range(NB):
                after(act, lg_done, tb - 1)
                copy(XH[:, tb % 2, :, :], x2T[:, :, tb * TB:(tb + 1) * TB]).then_inc(xh_rdy, 1)
                if tb >= 1:
                    act.wait_ge(lg_done, tb)
                    copy(lgT[:, (tb - 1) * TB:tb * TB], lg_ps[(tb - 1) % 2][0:E, :]).then_inc(lg_rdy, 1)
            act.wait_ge(lg_done, NB)
            copy(lgT[:, (NB - 1) * TB:NB * TB], lg_ps[(NB - 1) % 2][0:E, :]).then_inc(lg_rdy, 1)
            act.wait_ge(ex_rdy, 1)
            nc.scalar.activation(ex[:], ex[:], ACT.Exp).then_inc(soft_e, 1)
            for n in range(NB):
                act.wait_ge(wdT_done, n + 1)
                copy(wdT[:, n * TB:(n + 1) * TB], tr_ps[n % 2][0:E, :]).then_inc(wdT_rdy, 1)
            act.wait_ge(z_rdy, 1)
            nc.scalar.activation(ex[:], ex[:], ACT.Exp).then_inc(z_exp, 1)
            for n in range(NB):
                act.wait_ge(sT_done, n + 1)
                copy(softT[:, n * TB:(n + 1) * TB], tr_ps[n % 2][0:E, :]).then_inc(sT_rdy, 1)
            act.wait_ge(sT_rdy, NB)
            copy(soft_h[:], softT[:]).then_inc(h_rdy, 1)

        @block.vector
        def _(dve):
            sub = lambda out, a, b: nc.vector.tensor_tensor(out, a, b, ALU.subtract)
            own = Steps(dve, steps, 0, 0)

            def do(instruction):
                own.did(instruction)
                own.settle()

            for tb in range(NB):
                dve.wait_ge(xh_rdy, tb + 1)
                sub(XL[:, tb % 2, :, :], x2T[:, :, tb * TB:(tb + 1) * TB], XH[:, tb % 2, :, :].bitcast(F32)).then_inc(xl_rdy, 1)
            dve.wait_ge(l_inv, 16)
            dve.wait_ge(iota_in, 1)
            own.did(nc.vector.tensor_copy(row[:], row_i[:]))
            do(nc.vector.tensor_copy(inv_f[:], inv_i[:]))
            do(nc.vector.tensor_scalar(neg[:], inv_f[:], 0.0, float(E), ALU.is_lt, ALU.mult))
            do(nc.vector.tensor_tensor(inv_f[:], inv_f[:], neg[:], ALU.add))
            do(nc.vector.tensor_scalar(sel[:], inv_f[:], row[:, 0:1], None, ALU.is_equal))
            do(nc.vector.memset(ext[:, :, E:E + 2], -1.0))

            dve.wait_ge(tok_done, 2)
            for i in range(2):
                last = nc.vector.tensor_copy(sc[:, 8 * i:8 * i + 8, :], tok_ps[i][:])
            do(last)
            do(nc.vector.reduce_max(col[:, :, 0:1], sc[:], AX_X))
            sub(ex[:], sc[:], col[:, :, 0:1].to_broadcast([P, NT, E])).then_inc(ex_rdy, 1)
            dve.wait_ge(soft_e, 1)
            do(nc.vector.reduce_sum(col[:, :, 0:1], ex[:], AX_X))
            do(nc.vector.reciprocal(col[:, :, 0:1], col[:, :, 0:1]))
            do(nc.vector.tensor_tensor(sc[:], ex[:], col[:, :, 0:1].to_broadcast([P, NT, E]), ALU.mult))
            do(nc.vector.tensor_copy(ext[:, :, 0:E], sc[:]))
            for i in range(NT):
                last = nc.vector.max(top[:, i, :], ext[:, i, 0:E])
            do(last)
            do(nc.vector.memset(top[:, :, TOPK:8], -1.0))
            for i in range(NT):
                last = nc.vector.match_replace(rest[:, i, :], top[:, i, :], ext[:, i, :], 0.0)
            do(last)
            sub(wd[:], sc[:], rest[:, :, 0:E]).then_inc(wd_rdy, 1)
            dve.wait_ge(flat_done, 2)
            for i in range(2):
                last = nc.vector.tensor_copy(flat[:, 8 * i:8 * i + 8, :], tok_ps[i][:])
            do(last)
            by_expert = lambda t: t[:].rearrange("p n (f k) -> p n f k", k=K8)
            do(nc.vector.tensor_reduce(scal[:], by_expert(flat), axis=AX_X, op=ALU.add))
            do(nc.vector.tensor_scalar(ex[:], flat[:], 0.0, -1e9, ALU.is_equal, ALU.mult))
            do(nc.vector.tensor_tensor(ex[:], ex[:], flat[:], ALU.add))
            do(nc.vector.tensor_reduce(col[:], by_expert(ex), axis=AX_X, op=ALU.max))
            cols = lambda c: c[:].unsqueeze(3).to_broadcast([P, NT, F, K8])
            sub(by_expert(ex), by_expert(ex), cols(col)).then_inc(z_rdy, 1)
            dve.wait_ge(z_exp, 1)
            do(nc.vector.tensor_reduce(col2[:], by_expert(ex), axis=AX_X, op=ALU.add))
            do(nc.vector.reciprocal(col2[:], col2[:]))
            nc.vector.tensor_tensor(by_expert(wd), by_expert(ex), cols(col2), ALU.mult).then_inc(soft_rdy, 1)
            dve.wait_ge(h_rdy, 1)
            sub(soft_l[:], softT[:], soft_h[:].bitcast(F32)).then_inc(l_rdy, 1)

        @block.tensor
        def _(pe):
            mm = nc.tensor.matmul
            for tb in range(NB):
                pe.wait_ge(xl_rdy, tb + 1)
                if tb >= 2:
                    pe.wait_ge(lg_rdy, tb - 1)
                for k in range(KC):
                    for n, (w, x) in enumerate(((GH, XH), (GH, XL), (GL, XH), (GL, XL))):
                        last = mm(lg_ps[tb % 2][0:E, :], w[:, k, :], x[:, tb % 2, k, :], start=(k == 0 and n == 0),
                                  stop=(k == KC - 1 and n == 3))
                last.then_inc(lg_done, 1)
            for i in range(NT):
                if i % 4 == 0:
                    pe.wait_ge(lg_rdy, i // 4 + 1)
                last = nc.tensor.transpose(tok_ps[i // 8][:, i % 8, :], lgT[:, i * P:(i + 1) * P], ident[0:E, 0:E])
                if i % 8 == 7:
                    last.then_inc(tok_done, 1)

            def to_rows(done, copied):
                for i in range(NT):
                    if i % 4 == 0 and i >= 8:
                        pe.wait_ge(copied, i // 4 - 1)
                    last = nc.tensor.transpose(tr_ps[i // 4 % 2][0:E, i % 4 * P:(i % 4 + 1) * P], wd[:, i, :], ident[:])
                    if i % 4 == 3:
                        last.then_inc(done, 1)

            pe.wait_ge(wd_rdy, 1)
            to_rows(wdT_done, wdT_rdy)
            for i in range(NT):
                if i % 4 == 0:
                    pe.wait_ge(wdT_rdy, i // 4 + 1)
                last = mm(tok_ps[i // 8][:, i % 8, :], wdT[:, i * P:(i + 1) * P], sel[:], start=True, stop=True)
                if i % 8 == 7:
                    last.then_inc(flat_done, 1)
            pe.wait_ge(soft_rdy, 1)
            to_rows(sT_done, sT_rdy)


class Landing:

    def __init__(self, nc, ctx, A):
        self.nc, self.A = nc, A
        self.gu = [ctx.enter_context(nc.sbuf_tensor(f"gu_raw{j}", [P, KC, 2, M], F32)) for j, M in enumerate(ITILES)]
        self.dw = ctx.enter_context(nc.sbuf_tensor("dw_raw", [P, NI, D], F32))
        self.l_gu = [ctx.enter_context(nc.semaphore(f"l_gu{j}")) for j in range(NI)]
        self.l_dw = ctx.enter_context(nc.semaphore("l_dw"))

    def load_gu(self, sp, e, j):
        at, M = KC * 2 * P * j, ITILES[j]
        sp.dma_start(self.gu[j][:].rearrange("p k s m -> p (k s m)"),
                     self.A["gu"][e, :, at:at + KC * 2 * M]).then_inc(self.l_gu[j], 16)

    def load_dw(self, sp, e):
        dw = self.A["dw"]
        sp.dma_start(self.dw[:, 0:NI - 1, :], dw[e, 0:(NI - 1) * P, :].rearrange("(j p) n -> p j n", p=P)).then_inc(self.l_dw, 16)
        sp.dma_start(self.dw[0:ITILES[-1], NI - 1, :], dw[e, (NI - 1) * P:I, :]).then_inc(self.l_dw, 16)

    def load_first(self, sp):
        for j in range(NI):
            self.load_gu(sp, 0, j)
        self.load_dw(sp, 0)


def experts(nc, A, landing, x2T, xtok, scal, soft_f, soft_hl):
    F32, F32R = mybir.dt.float32, mybir.dt.float32r
    with ExitStack() as ctx:
        def sb(name, shape, dt=F32):
            return ctx.enter_context(nc.sbuf_tensor(name, shape, dt))

        def sem(name):
            return ctx.enter_context(nc.semaphore(name))

        MUS = sb("MUS", [72, D], F32R)
        QAH, QAL = sb("QAH", [P, KC, P], F32R), sb("QAL", [P, KC, P], F32R)
        GUH = [sb(f"GUH{j}", [P, KC, 2, M], F32R) for j, M in enumerate(ITILES)]
        GUL = [sb(f"GUL{j}", [P, KC, 2, M], F32R) for j, M in enumerate(ITILES)]
        QBH, QBL = sb("QBH", [P, 2, I], F32R), sb("QBL", [P, I], F32R)
        QDH, QDL = sb("QDH", [P, NI, KR], F32R), sb("QDL", [P, NI, KR], F32R)
        DWH, DWL = sb("DWH", [P, NI, D], F32R), sb("DWL", [P, NI, D], F32R)
        DBH, DBL = sb("DBH", [P, D], F32R), sb("DBL", [KR, D], F32R)
        mu_raw, qa_raw = sb("mu_raw", [72, D]), sb("qa_raw", [P, KC, P])
        gu_raw, dw_raw, l_gu, l_dw = landing.gu, landing.dw, landing.l_gu, landing.l_dw
        qb_raw, qb_scale = sb("qb_raw", [P, 2, I]), sb("qb_scale", [P, 2, I])
        qd_raw = sb("qd_raw", [P, NI, KR])
        db_raw, db_scale = sb("db_raw", [P, D]), sb("db_scale", [P, D])
        XH, XL = sb("XH", [P, KC, TB], F32R), sb("XL", [P, KC, TB], F32R)
        xe = sb("xe", [P, 2, TB])
        HH, HL = sb("HH", [P, NI, TB], F32R), sb("HL", [P, NI, TB], F32R)
        h = sb("h", [P, 2, TB])
        sg = sb("sg", [P, 2, TB])
        low = sb("low", [P, TB])
        G2, U2, D2 = sb("G2", [P, TB], F32R), sb("U2", [P, TB], F32R), sb("D2", [P, TB], F32R)
        wrep = sb("wrep", [P, 2, TB])
        ws = sb("ws", [72, 2, TB], F32R)
        sf = sb("sf", [P, NT])
        st, mv, ve, rstd, half = sb("f_st", [P, 4, 6]), sb("f_mv", [P, 4, 2]), sb("f_ve", [P, 4]), sb("f_rstd", [P, 4]), sb("f_half", [P, 4])

        pair = [[ctx.enter_context(nc.psum_tensor(f"pair{b}{s}", [P, TB], F32)) for s in range(2)] for b in range(2)]
        qa_ps = ctx.enter_context(nc.psum_tensor("qa_ps", [P, TB], F32))
        qd_ps = ctx.enter_context(nc.psum_tensor("qd_ps", [P, TB], F32))
        y_ps = [ctx.enter_context(nc.psum_tensor(f"y_ps{b}", [P, D], F32)) for b in range(2)]

        l_mu, l_qa, l_qb, l_qd, l_db = (sem(n) for n in ("l_mu", "l_qa", "l_qb", "l_qd", "l_db"))
        l_wrep, l_ws = [sem(f"l_wrep{b}") for b in range(2)], [sem(f"l_ws{b}") for b in range(2)]
        qb_scaled, db_scaled = sem("qb_scaled"), sem("db_scaled")
        gu_hi, dw_hi, lr_hi = sem("gu_hi"), sem("dw_hi"), sem("lr_hi")
        w_gu, w_dw, w_mu, w_qa, w_qb, w_qd, w_db = (sem(n) for n in ("w_gu", "w_dw", "w_mu", "w_qa", "w_qb", "w_qd", "w_db"))
        zeroed = sem("zeroed")
        xe_done, qa_done, gu_done, qd_done, y_done = (sem(n) for n in ("xe_done", "qa_done", "gu_done", "qd_done", "y_done"))
        xe_rdy, xh_rdy, xl_rdy = sem("xe_rdy"), sem("xh_rdy"), sem("xl_rdy")
        low_rdy, gu2_hi, gu2_rdy, d2_hi, d2_rdy = (sem(n) for n in ("low_rdy", "gu2_hi", "gu2_rdy", "d2_hi", "d2_rdy"))
        lowd_rdy = sem("lowd_rdy")
        silu_rdy, h_rdy, hh_rdy, hl_rdy, y_added, sf_rdy = (sem(n) for n in ("silu_rdy", "h_rdy", "hh_rdy", "hl_rdy", "y_added", "sf_rdy"))
        stats, ve_rdy, rstd_rdy, out_rdy, stored = (sem("f_" + n) for n in ("stats", "ve_rdy", "rstd_rdy", "out_rdy", "stored"))
        block = ctx.enter_context(nc.Block())

        def over_experts(eng, body):
            body(0, False, False)
            body(1, False, True)
            body(2, True, True)
            with eng.Fori(3, 1 + NF) as e:
                body(e, True, True)
            body(1 + NF, True, None)

        def slot(tb, j):
            return (NI * tb + j) % 2

        @block.sync
        def _(sp):
            def load(e, routed):
                f = e - 2
                for j in range(NI):
                    after(sp, w_gu, NI * (e - 1) + j + 1)
                    landing.load_gu(sp, e, j)
                after(sp, w_dw, e)
                landing.load_dw(sp, e)
                if not routed:
                    return
                after(sp, w_mu, f)
                sp.wait_ge(zeroed, 1)
                for r in (0, 32, 64):
                    sp.dma_start(mu_raw[r:r + K8, :], A["mu"][f, :, :]).then_inc(l_mu, 16)
                after(sp, w_qa, f)
                sp.dma_start(qa_raw[:].rearrange("p k m -> p (k m)"), A["qa"][f, :, :]).then_inc(l_qa, 16)
                after(sp, w_qb, f)
                for r in (0, KR):
                    sp.dma_start(qb_raw[r:r + KR, :, :], A["qb"][f, :, :, :]).then_inc(l_qb, 16)
                sp.dma_start(qb_scale[:].rearrange("p s i -> p (s i)"),
                             A["gu_scale"][f, :].partition_broadcast(P)).then_inc(l_qb, 16)
                after(sp, w_qd, f)
                sp.dma_start(qd_raw[:, 0:NI - 1, :], A["qd"][f, 0:(NI - 1) * P, :].rearrange("(j p) n -> p j n", p=P)).then_inc(l_qd, 16)
                sp.dma_start(qd_raw[0:ITILES[-1], NI - 1, :], A["qd"][f, (NI - 1) * P:I, :]).then_inc(l_qd, 16)
                after(sp, w_db, f)
                for r in (0, KR):
                    sp.dma_start(db_raw[r:r + KR, :], A["db"][f, :, :]).then_inc(l_db, 16)
                sp.dma_start(db_scale[:], A["d_scale"][f, :].partition_broadcast(P)).then_inc(l_db, 16)

            def load_ws(f, tb):
                n = f * NB + tb
                b = tb % 2
                sp.wait_ge(zeroed, 2)
                after(sp, xe_done, KC * (n - 1))
                for r, part in ((0, 0), (32, 1), (64, 0)):
                    sp.dma_start(ws[r:r + K8, b, :].bitcast(F32),
                                 soft_hl[part, f, :, tb * TB:(tb + 1) * TB]).then_inc(l_ws[b], 16)

            def load_wrep(f, tb):
                n = f * NB + tb
                b = tb % 2
                after(sp, lowd_rdy, n - 1)
                for s in range(2):
                    sp.dma_start(wrep[s * KR:(s + 1) * KR, b, :],
                                 soft_f[f, :, tb * TB:(tb + 1) * TB].unsqueeze(1).to_broadcast([K8, R8, TB])).then_inc(l_wrep[b], 16)

            def body(e, routed, nxt):
                f = e - 2
                for tb in range(NB):
                    if (routed and tb < NB - 1) or (nxt and tb == NB - 1):
                        load_wrep(f + (tb + 1) // NB, (tb + 1) % NB)
                    if (routed and tb < NB - 2) or (nxt and tb >= NB - 2):
                        load_ws(f + (tb + 2) // NB, (tb + 2) % NB)
                    if tb == 0 and nxt is not None:
                        load(e + 1, nxt)
                    if nxt is None and tb >= 1:
                        store(tb - 1)

            def store(tb):
                sp.wait_ge(out_rdy, 4 * (tb + 1))
                sp.dma_start(A["out"][tb * TB:(tb + 1) * TB, :].rearrange("(i p) n -> p i n", p=P),
                             xtok[:, 4 * tb:4 * tb + 4, :]).then_inc(stored, 16)

            over_experts(sp, body)
            store(NB - 1)
            sp.wait_ge(stored, 16 * NB)

        @block.gpsimd
        def _(pool):
            nc.gpsimd.memset(mu_raw[:], 0.0).then_inc(zeroed, 1)
            nc.gpsimd.memset(ws[:].bitcast(F32), 0.0).then_inc(zeroed, 1)
            nc.gpsimd.memset(half[:], -0.5).then_inc(zeroed, 1)
            pool.wait_ge(zeroed, 3)

            def body(e, routed, nxt):
                f = e - 2
                for tb in range(NB):
                    if nxt and tb == NB - 2:
                        pool.wait_ge(l_qb, 48 * (f + 2))
                        nc.gpsimd.tensor_tensor(qb_raw[:], qb_raw[:], qb_scale[:], ALU.mult).then_inc(qb_scaled, 1)
                        pool.wait_ge(l_db, 48 * (f + 2))
                        nc.gpsimd.tensor_tensor(db_raw[:], db_raw[:], db_scale[:], ALU.mult).then_inc(db_scaled, 1)
                    if nxt is None:
                        pool.wait_ge(ve_rdy, tb + 1)
                        nc.gpsimd.tensor_tensor(rstd[:], ve[:], half[:], ALU.pow).then_inc(rstd_rdy, 1)
            over_experts(pool, body)

        @block.scalar
        def _(act):
            copy = lambda out, src: nc.scalar.activation(out, src, ACT.Copy)

            def gu_split(e, j):
                act.wait_ge(l_gu[j], 16 * (e + 1))
                after(act, gu_done, NI * NB * (e - 1) + NI * (NB - 1) + j + 1)
                copy(GUH[j][:], gu_raw[j][:]).then_inc(gu_hi, 1)

            def dw_split(e):
                act.wait_ge(l_dw, 32 * (e + 1))
                after(act, y_done, NB * 4 * e)
                copy(DWH[:, 0:NI - 1, :], dw_raw[:, 0:NI - 1, :])
                copy(DWH[0:ITILES[-1], NI - 1, :], dw_raw[0:ITILES[-1], NI - 1, :]).then_inc(dw_hi, 1)

            for k in range(KC):
                copy(XH[:, k, :], x2T[:, k, 0:TB]).then_inc(xh_rdy, 1)
            gu_split(0, 0), gu_split(0, 1), gu_split(0, 2), dw_split(0)

            def body(e, routed, nxt):
                f = e - 2
                for tb in range(NB):
                    s, n = e * NB + tb, f * NB + tb
                    turn = tb == NB - 1 and nxt is not None
                    if turn and nxt:
                        act.wait_ge(l_mu, 48 * (f + 2))
                        after(act, xe_done, KC * (n + 1))
                        copy(MUS[:], mu_raw[:]).then_inc(lr_hi, 1)
                    if routed:
                        act.wait_ge(low_rdy, n + 1)
                        copy(G2[0:KR, :], low[0:KR, :]).then_inc(gu2_hi, 1)
                        copy(U2[KR:P, :], low[KR:P, :]).then_inc(gu2_hi, 1)
                    if turn and nxt:
                        act.wait_ge(l_qa, 16 * (f + 2))
                        after(act, qa_done, n + 1)
                        copy(QAH[:], qa_raw[:]).then_inc(lr_hi, 1)
                    for j, M in enumerate(ITILES):
                        b = slot(tb, j)
                        act.wait_ge(gu_done, NI * s + j + 1)
                        nc.scalar.activation(sg[0:M, b, :], pair[b][0][0:M, :], ACT.Silu).then_inc(silu_rdy, 1)
                        act.wait_ge(h_rdy, NI * s + j + 1)
                        copy(HH[0:M, j, :], h[0:M, b, :]).then_inc(hh_rdy, 1)
                        if turn and j < NI - 1:
                            gu_split(e + 1, j)
                    def next_x(k):
                        m = f * NB + tb + 1
                        if routed or turn and nxt:
                            act.wait_ge(xe_rdy, KC * m + k + 1)
                            copy(XH[:, k, :], xe[:, k % 2, :]).then_inc(xh_rdy, 1)
                        else:
                            t = (tb + 1) % NB * TB
                            copy(XH[:, k, :], x2T[:, k, t:t + TB]).then_inc(xh_rdy, 1)
                    more = tb < NB - 1 or nxt is not None
                    if more:
                        next_x(0), next_x(1)
                    if routed:
                        act.wait_ge(lowd_rdy, n + 1)
                        copy(D2[0:KR, :], low[0:KR, :]).then_inc(d2_hi, 1)
                    if more:
                        next_x(2), next_x(3)
                    if turn and nxt:
                        act.wait_ge(qb_scaled, f + 2)
                        copy(QBH[:], qb_raw[:]).then_inc(lr_hi, 1)
                    if turn:
                        gu_split(e + 1, NI - 1)
                    if turn and nxt:
                        act.wait_ge(l_qd, 32 * (f + 2))
                        after(act, qd_done, n + 1)
                        copy(QDH[:, 0:NI - 1, :], qd_raw[:, 0:NI - 1, :])
                        copy(QDH[0:ITILES[-1], NI - 1, :], qd_raw[0:ITILES[-1], NI - 1, :]).then_inc(lr_hi, 1)
                    if turn:
                        dw_split(e + 1)
                        if nxt:
                            act.wait_ge(db_scaled, f + 2)
                            copy(DBH[:], db_raw[:]).then_inc(lr_hi, 1)
            over_experts(act, body)

        @block.vector
        def _(dve):
            sub = lambda out, a, b: nc.vector.tensor_tensor(out, a, b, ALU.subtract)

            def gu_split(e, j):
                dve.wait_ge(gu_hi, NI * e + j + 1)
                sub(GUL[j][:], gu_raw[j][:], GUH[j][:].bitcast(F32)).then_inc(w_gu, 1)

            def dw_split(e):
                dve.wait_ge(dw_hi, e + 1)
                sub(DWL[:, 0:NI - 1, :], dw_raw[:, 0:NI - 1, :], DWH[:, 0:NI - 1, :].bitcast(F32))
                M = ITILES[-1]
                sub(DWL[0:M, NI - 1, :], dw_raw[0:M, NI - 1, :], DWH[0:M, NI - 1, :].bitcast(F32)).then_inc(w_dw, 1)

            for k in range(KC):
                dve.wait_ge(xh_rdy, k + 1)
                sub(XL[:, k, :], x2T[:, k, 0:TB], XH[:, k, :].bitcast(F32)).then_inc(xl_rdy, 1)
            gu_split(0, 0), gu_split(0, 1), gu_split(0, 2), dw_split(0)

            def norm_block(e, tb):
                dve.wait_ge(y_added, 4 * (e * NB + tb) + 4)
                for i in range(4):
                    done = nc.vector.bn_stats(st[:, i, :], xtok[:, 4 * tb + i, :])
                done.then_inc(stats, 1)
                dve.wait_ge(stats, 2 * tb + 1)
                for i in range(4):
                    done = nc.vector.bn_aggr(mv[:, i, :], st[:, i, :])
                done.then_inc(stats, 1)
                dve.wait_ge(stats, 2 * tb + 2)
                nc.vector.tensor_scalar(ve[:].unsqueeze(2), mv[:, :, 1:2], EPS, None, ALU.add).then_inc(ve_rdy, 1)
                dve.wait_ge(rstd_rdy, tb + 1)
                for i in range(4):
                    row = xtok[:, 4 * tb + i, :]
                    nc.vector.tensor_scalar(row, row, mv[:, i, 0:1], rstd[:, i:i + 1], ALU.subtract, ALU.mult).then_inc(out_rdy, 1)

            def body(e, routed, nxt):
                f = e - 2
                if routed:
                    dve.wait_ge(y_added, 4 * NB * e)
                    nc.vector.tensor_copy(sf[:].unsqueeze(2), scal[:, :, bass.ds(f, 1)]).then_inc(sf_rdy, 1)
                for tb in range(NB):
                    s, n = e * NB + tb, f * NB + tb
                    turn = tb == NB - 1 and nxt is not None
                    hi = 5 * (f + 1)
                    if turn and nxt:
                        dve.wait_ge(lr_hi, hi + 1)
                        sub(MUS[64:72, :], mu_raw[64:72, :], MUS[64:72, :].bitcast(F32)).then_inc(w_mu, 1)
                    if routed:
                        dve.wait_ge(qa_done, n + 1)
                        dve.wait_ge(l_wrep[tb % 2], 32 * (2 * f + tb // 2 + 1))
                        after(dve, d2_rdy, n)
                        nc.vector.tensor_tensor(low[:], qa_ps[:], wrep[:, tb % 2, :], ALU.mult).then_inc(low_rdy, 1)
                        dve.wait_ge(gu2_hi, 2 * n + 1)
                        sub(G2[KR:P, :], low[0:KR, :], G2[0:KR, :].bitcast(F32)).then_inc(gu2_rdy, 1)
                        dve.wait_ge(gu2_hi, 2 * n + 2)
                        sub(U2[0:KR, :], low[KR:P, :], U2[KR:P, :].bitcast(F32)).then_inc(gu2_rdy, 1)
                    if turn and nxt:
                        dve.wait_ge(lr_hi, hi + 2)
                        sub(QAL[:], qa_raw[:], QAH[:].bitcast(F32)).then_inc(w_qa, 1)
                    for j, M in enumerate(ITILES):
                        b = slot(tb, j)
                        dve.wait_ge(silu_rdy, NI * s + j + 1)
                        nc.vector.tensor_tensor(h[0:M, b, :], pair[b][1][0:M, :], sg[0:M, b, :], ALU.mult).then_inc(h_rdy, 1)
                        dve.wait_ge(hh_rdy, NI * s + j + 1)
                        sub(HL[0:M, j, :], h[0:M, b, :], HH[0:M, j, :].bitcast(F32)).then_inc(hl_rdy, 1)
                        if nxt is None and tb >= 1 and j == 0:
                            norm_block(e, tb - 1)
                        if turn and j < NI - 1:
                            gu_split(e + 1, j)

                    m, sm = n + 1, s + 1
                    t = (tb + 1) % NB * TB
                    more = tb < NB - 1 or nxt is not None

                    mixed = routed or turn and nxt

                    def next_sum(ks):
                        if more and mixed:
                            for k in ks:
                                dve.wait_ge(xe_done, KC * m + k + 1)
                                after(dve, xl_rdy, KC * sm + k - 1)
                                nc.vector.tensor_tensor(xe[:, k % 2, :], pair[slot(tb, 1 + k // 2)][k % 2][:],
                                                        x2T[:, k, t:t + TB], ALU.add).then_inc(xe_rdy, 1)

                    def next_low(k):
                        if more:
                            dve.wait_ge(xh_rdy, KC * sm + k + 1)
                            src = xe[:, k % 2, :] if mixed else x2T[:, k, t:t + TB]
                            sub(XL[:, k, :], src, XH[:, k, :].bitcast(F32)).then_inc(xl_rdy, 1)

                    def add_rows(i):
                        dve.wait_ge(y_done, 4 * s + i + 1)
                        acc = xtok[:, 4 * tb + i, :]
                        if i == 0 and routed:
                            dve.wait_ge(sf_rdy, f + 1)
                        after(dve, y_added, 4 * s + i + 1 - 4 * NB)
                        if routed:
                            nc.vector.scalar_tensor_tensor(acc, y_ps[i % 2][:], sf[:, 4 * tb + i:4 * tb + i + 1], acc,
                                                           ALU.mult, ALU.add).then_inc(y_added, 1)
                        else:
                            nc.vector.tensor_tensor(acc, y_ps[i % 2][:], acc, ALU.add).then_inc(y_added, 1)

                    next_sum((0, 1))
                    if routed:
                        dve.wait_ge(qd_done, n + 1)
                        dve.wait_ge(gu2_rdy, 2 * n + 2)
                        nc.vector.tensor_tensor(low[0:KR, :], qd_ps[0:KR, :], wrep[0:KR, tb % 2, :], ALU.mult).then_inc(lowd_rdy, 1)
                        dve.wait_ge(d2_hi, n + 1)
                        sub(D2[KR:P, :], low[0:KR, :], D2[0:KR, :].bitcast(F32)).then_inc(d2_rdy, 1)
                    next_low(0)
                    add_rows(0)
                    next_low(1)
                    add_rows(1)
                    next_sum((2, 3))
                    next_low(2)
                    next_low(3)
                    add_rows(2)
                    add_rows(3)
                    if nxt is None and tb == NB - 1:
                        norm_block(e, tb)
                    if turn and nxt:
                        dve.wait_ge(lr_hi, hi + 3)
                        sub(QBL[0:KR, :], qb_raw[0:KR, 0, :], QBH[0:KR, 0, :].bitcast(F32))
                        sub(QBL[KR:P, :], qb_raw[KR:P, 1, :], QBH[KR:P, 1, :].bitcast(F32)).then_inc(w_qb, 1)
                    if turn:
                        gu_split(e + 1, NI - 1)
                    if turn and nxt:
                        M = ITILES[-1]
                        dve.wait_ge(lr_hi, hi + 4)
                        sub(QDL[:, 0:NI - 1, :], qd_raw[:, 0:NI - 1, :], QDH[:, 0:NI - 1, :].bitcast(F32))
                        sub(QDL[0:M, NI - 1, :], qd_raw[0:M, NI - 1, :], QDH[0:M, NI - 1, :].bitcast(F32)).then_inc(w_qd, 1)
                    if turn:
                        dw_split(e + 1)
                        if nxt:
                            dve.wait_ge(lr_hi, hi + 5)
                            sub(DBL[:], db_raw[0:KR, :], DBH[0:KR, :].bitcast(F32)).then_inc(w_db, 1)
            over_experts(dve, body)

        @block.tensor
        def _(pe):
            mm = nc.tensor.matmul

            def three(out, wh, wl, xh, xl, first, last):
                mm(out, wh, xh, start=first, stop=False)
                mm(out, wh, xl, start=False, stop=False)
                return mm(out, wl, xh, start=False, stop=last)

            def XE(f, tb, at, k):
                if k == 0:
                    pe.wait_ge(w_mu, f + 1)
                    pe.wait_ge(l_ws[tb % 2], 48 * (2 * f + tb // 2 + 1))
                mm(pair[slot(at, 1 + k // 2)][k % 2][:], MUS[:, k * P:(k + 1) * P], ws[:, tb % 2, :],
                   start=True, stop=True).then_inc(xe_done, 1)

            def body(e, routed, nxt):
                f = e - 2
                for tb in range(NB):
                    s, n = e * NB + tb, f * NB + tb
                    more = tb < NB - 1 or nxt is not None
                    mixed_next = (routed and tb < NB - 1) or (nxt and tb == NB - 1)
                    pe.wait_ge(xl_rdy, KC * (s + 1))
                    if routed:
                        pe.wait_ge(w_qa, f + 1)
                        after(pe, low_rdy, n)
                        for k in range(KC):
                            last = three(qa_ps[:], QAH[:, k, :], QAL[:, k, :], XH[:, k, :], XL[:, k, :], k == 0, k == KC - 1)
                        last.then_inc(qa_done, 1)
                    for j, M in enumerate(ITILES):
                        b = slot(tb, j)
                        after(pe, h_rdy, NI * s + j - 1)
                        pe.wait_ge(w_gu, NI * e + j + 1)
                        for c in range(2):
                            for k in range(KC):
                                last = three(pair[b][c][0:M, :], GUH[j][:, k, c, :], GUL[j][:, k, c, :],
                                             XH[:, k, :], XL[:, k, :], k == 0, k == KC - 1 and not routed)
                        if routed:
                            if j == 0:
                                pe.wait_ge(w_qb, f + 1)
                                pe.wait_ge(gu2_rdy, 2 * n + 2)
                            cols = slice(j * P, j * P + M)
                            for c, S2, hi in ((0, G2, slice(0, KR)), (1, U2, slice(KR, P))):
                                mm(pair[b][c][0:M, :], QBH[:, c, cols], S2[:], start=False, stop=False)
                                last = mm(pair[b][c][0:M, :], QBL[hi, cols], S2[hi, :], start=False, stop=True)
                        last.then_inc(gu_done, 1)

                    def down(i, js, first=False, stop=False):
                        out = y_ps[i % 2][:]
                        t = slice(i * P, (i + 1) * P)
                        if first:
                            after(pe, y_added, 4 * s + i - 1)
                        for j in js:
                            M = ITILES[j]
                            pe.wait_ge(hl_rdy, NI * s + j + 1)
                            last = three(out, HH[0:M, j, t], HL[0:M, j, t], DWH[0:M, j, :], DWL[0:M, j, :],
                                         first and j == js[0], stop and j == js[-1])
                        return last

                    def down_low(i):
                        out = y_ps[i % 2][:]
                        t = slice(i * P, (i + 1) * P)
                        mm(out, D2[:, t], DBH[:], start=False, stop=False)
                        mm(out, D2[0:KR, t], DBL[:], start=False, stop=True).then_inc(y_done, 1)

                    def finish(i, js, first=False):
                        last = down(i, js, first, not routed)
                        if routed:
                            down_low(i)
                        else:
                            last.then_inc(y_done, 1)

                    pe.wait_ge(w_dw, e + 1)
                    down(0, (0, 1), True)
                    if mixed_next:
                        pe.wait_ge(h_rdy, NI * s + 2)
                        XE(f + (tb + 1) // NB, (tb + 1) % NB, tb, 0)
                        XE(f + (tb + 1) // NB, (tb + 1) % NB, tb, 1)
                    if routed:
                        pe.wait_ge(w_qd, f + 1)
                        after(pe, lowd_rdy, n)
                        for j, M in enumerate(ITILES):
                            pe.wait_ge(hl_rdy, NI * s + j + 1)
                            last = three(qd_ps[0:KR, :], QDH[0:M, j, :], QDL[0:M, j, :], HH[0:M, j, :], HL[0:M, j, :],
                                         j == 0, j == NI - 1)
                        last.then_inc(qd_done, 1)
                    if mixed_next:
                        pe.wait_ge(h_rdy, NI * s + 3)
                        XE(f + (tb + 1) // NB, (tb + 1) % NB, tb, 2)
                        XE(f + (tb + 1) // NB, (tb + 1) % NB, tb, 3)
                    if routed:
                        down(0, (2,))
                        down(1, (0, 1), True)
                        pe.wait_ge(w_db, f + 1)
                        pe.wait_ge(d2_rdy, n + 1)
                        down_low(0)
                        down(1, (2,))
                        down_low(1)
                    else:
                        down(1, (0, 1), True)
                        finish(0, (2,))
                        finish(1, (2,))
                    finish(2, (0, 1, 2), True)
                    finish(3, (0, 1, 2), True)
            over_experts(pe, body)


def program(nc, A):
    with ExitStack() as ctx:
        x2T = ctx.enter_context(nc.sbuf_tensor("x2T", [P, KC, T], F32))
        xtok = ctx.enter_context(nc.sbuf_tensor("xtok", [P, NT, D], F32))
        scal = ctx.enter_context(nc.sbuf_tensor("scal", [P, NT, F], F32))
        soft_f = nc.dram_tensor("soft_f", [F, K8, T], F32).ap()
        soft_hl = nc.dram_tensor("soft_hl", [2, F, K8, T], F32).ap()
        splitter = Splitter(nc, ctx)
        ident = ctx.enter_context(nc.sbuf_tensor("ident", [P, P], F32))
        with nc.semaphore("ident_rdy") as ident_rdy, nc.Block() as block:
            @block.gpsimd
            def _(pool):
                nc.gpsimd.memset(ident[:], 0.0).then_inc(ident_rdy, 1)
                pool.wait_ge(ident_rdy, 1)
                nc.gpsimd.affine_select(out=ident[:], in_=ident[:], compare_op=ALU.not_equal, fill=1.0,
                                        base=0, pattern=[[-1, P]], channel_multiplier=1)
        with nc.sbuf_tensor("bo_rows", [P, D], F32) as bo:
            attention(nc, splitter, A, ident, bo, x2T, xtok)
        cross(nc, splitter, A, ident, x2T, xtok)
        landing = Landing(nc, ctx, A)
        gating(nc, splitter, A, ident, x2T, scal, soft_f, soft_hl, landing.load_first)
        experts(nc, A, landing, x2T, xtok, scal, soft_f, soft_hl)


def lay_out(inputs):
    import numpy as np

    a = {n: np.asarray(v) for n, v in inputs.items()}
    ffn = lambda n: a["L0_ffn_" + n]
    by_chunk = lambda w: w.reshape(KC, P, -1).transpose(1, 0, 2)
    tokens = a["x"].reshape(T, D)
    out = {
        "x": tokens,
        "xT": tokens.reshape(T, KC, P).transpose(2, 1, 0),
        "cT": a["ctx_2048"].reshape(T, KC, P).transpose(2, 1, 0),
        "wq": by_chunk(a["L0_attn_Wq"].reshape(D, KV, G, HD).transpose(0, 2, 1, 3).reshape(D, D)),
        "wk": by_chunk(a["L0_attn_Wk"]),
        "wv": by_chunk(a["L0_attn_Wv"]),
        "wo": by_chunk(a["L0_attn_Wo"].reshape(KV, G, HD, D).transpose(1, 0, 2, 3).reshape(D, D)),
        "xb": np.stack([a["L0_xattn_b" + n].reshape(KC, P) for n in "qkv"]).transpose(2, 0, 1),
        "xbo": a["L0_xattn_bo"],
        "gate": by_chunk(ffn("gate_weight").T),
        "inv": ffn("inv_mapping").reshape(E),
    }
    for n in "qkvo":
        out["xw" + n] = by_chunk(a["L0_xattn_W" + n].T)
    pair = np.stack([np.concatenate([ffn("sh_gate_W").reshape(2, I, D), ffn("gate_W")]),
                     np.concatenate([ffn("sh_up_W").reshape(2, I, D), ffn("up_W")])])
    pair = pair.reshape(2, 2 + F, I, KC, P).transpose(1, 4, 3, 0, 2)
    out["gu"] = np.concatenate([pair[..., j * P:j * P + m].reshape(2 + F, P, -1) for j, m in enumerate(ITILES)], axis=2)
    out["dw"] = np.concatenate([ffn("sh_down_W").T.reshape(2, I, D), ffn("down_W").transpose(0, 2, 1)])
    out["mu"] = ffn("mask_up_W").transpose(0, 2, 1)
    out["qa"] = np.stack([ffn("gate_qa"), ffn("up_qa")], axis=1).reshape(F, P, KC, P).transpose(0, 3, 2, 1).reshape(F, P, D)
    out["qb"] = np.stack([ffn("gate_qb"), ffn("up_qb")], axis=1).transpose(0, 2, 4, 1, 3).reshape(F, KR, 2, I)
    out["gu_scale"] = np.stack([ffn("gate_scale"), ffn("up_scale")], axis=1).reshape(F, 2 * I)
    out["qd"] = ffn("down_qa").reshape(F, KR, I).transpose(0, 2, 1)
    out["db"] = ffn("down_qb").transpose(0, 1, 3, 2).reshape(F, KR, D)
    out["d_scale"] = ffn("down_scale")
    return {n: np.ascontiguousarray(v) for n, v in out.items()}


def kernel(**inputs):
    import concourse.bacc as bacc
    from concourse.bass_utils import run_bass_kernel_spmd

    nc = bacc.Bacc("TRN2", target_bir_lowering=False, num_devices=1)
    arrays = lay_out(inputs)
    A = {n: nc.dram_tensor("in_" + n, v.shape, mybir.dt.from_np(v.dtype), kind="ExternalInput").ap() for n, v in arrays.items()}
    A["out"] = nc.dram_tensor("out", (T, D), F32, kind="ExternalOutput").ap()
    program(nc, A)
    r = run_bass_kernel_spmd(nc, [{"in_" + n: v for n, v in arrays.items()}], core_ids=[0])
    return r.results[0]["out"].reshape(B, S, D)
```
